# Optimizing a Trainium2 kernel written in Bass

```python
import numpy as np
import jax
import jax.numpy as jnp

def _softmax(x, axis=-1):
    return jax.nn.softmax(x, axis=axis)

def _gelu(x):
    return jax.nn.gelu(x, approximate=True)

def _silu(x):
    return jax.nn.silu(x)

def _sigmoid(x):
    return jax.nn.sigmoid(x)

def _layernorm(x, axis=-1, eps=1e-05):
    m = jnp.mean(x, axis=axis, keepdims=True)
    v = jnp.var(x, axis=axis, keepdims=True)
    return (x - m) / jnp.sqrt(v + eps)

def _scatter_add(tgt, idx, src, axis=0):
    return tgt.at[idx].add(src)

def _segment_sum(src, seg, n):
    return jax.ops.segment_sum(src, seg, n)
kernel_name = 'mk_gnn_preln_d2_gnn_r32_90ac50'

def setup_inputs(seed: int=0):
    np.random.seed(seed)
    _w = jnp.asarray

    def _rec_inputs():
        import jax
        import jax.numpy as jnp
        _gk = jax.random.key(seed)
        x = -0.000202 + 1 * jax.random.normal(jax.random.fold_in(_gk, 1), (3125, 128), jnp.float32)
        src = jax.random.randint(jax.random.fold_in(_gk, 2), (50000,), 0, 3125, jnp.int32)
        dst = jax.random.randint(jax.random.fold_in(_gk, 3), (50000,), 0, 3125, jnp.int32)
        _o = jnp.argsort(dst, stable=True)
        src = src[_o]
        dst = dst[_o]
        return (x, src, dst)
    x, src, dst = _rec_inputs()

    def _L0_gnn_setup():
        import jax, jax.numpy as jnp
        import numpy as np
        N, E = (50000, 25000)
        D_IN, D_HID, D_OUT = (128, 256, 128)

        def _sage_layer(h, edge_src, edge_dst, W, b, inv_deg):
            msgs = h[edge_src]
            agg = jax.ops.segment_sum(msgs, edge_dst, num_segments=h.shape[0]) * inv_deg
            y = jnp.concatenate([h, agg], axis=1)
            return y @ W + b
        key = jax.random.key(seed)
        k = jax.random.split(key, 7)
        x = jax.random.normal(k[0], (N, D_IN), dtype=jnp.float32)
        edge_src = jax.random.randint(k[1], (E,), 0, N, dtype=jnp.int32)
        edge_dst = jax.random.randint(k[2], (E,), 0, N, dtype=jnp.int32)
        s1 = 1.0 / np.sqrt(2 * D_IN)
        s2 = 1.0 / np.sqrt(2 * D_HID)
        W1 = jax.random.uniform(k[3], (2 * D_IN, D_HID), jnp.float32, -s1, s1)
        b1 = jax.random.uniform(k[4], (D_HID,), jnp.float32, -s1, s1)
        W2 = jax.random.uniform(k[5], (2 * D_HID, D_OUT), jnp.float32, -s2, s2)
        b2 = jax.random.uniform(k[6], (D_OUT,), jnp.float32, -s2, s2)
        return {'x': x, 'edge_src': edge_src, 'edge_dst': edge_dst, 'W1': W1, 'b1': b1, 'W2': W2, 'b2': b2}
    _L0_gnn_all = _L0_gnn_setup()
    _L0_gnn_in = {k: v for k, v in _L0_gnn_all.items() if k in ('W1', 'b1', 'W2', 'b2')}
    del _L0_gnn_all

    def _L1_gnn_setup():
        import jax, jax.numpy as jnp
        import numpy as np

        def _sage_conv(x, src, dst, W_l, b_l, W_r, n_nodes):
            msgs = x[src]
            agg = jax.ops.segment_sum(msgs, dst, num_segments=n_nodes)
            deg = jax.ops.segment_sum(jnp.ones((src.shape[0],), x.dtype), dst, num_segments=n_nodes)
            mean = agg / jnp.clip(deg, 1.0)[:, None]
            return mean @ W_l.T + b_l + x @ W_r.T
        key = jax.random.key(seed)
        ks = jax.random.split(key, 10)
        N, E, F_IN, H, C = (50000, 25000, 128, 256, 128)

        def lin(k, o, i):
            return jax.random.normal(k, (o, i), jnp.float32) / np.sqrt(i).astype(np.float32)
        return {'x': jax.random.normal(ks[0], (N, F_IN), jnp.float32), 'edge_index': jax.random.randint(ks[1], (2, E), 0, N, dtype=jnp.int64) if jax.config.jax_enable_x64 else jax.random.randint(ks[1], (2, E), 0, N, dtype=jnp.int32), 'W_l0': lin(ks[2], H, F_IN), 'b_l0': jnp.zeros((H,), jnp.float32), 'W_r0': lin(ks[3], H, F_IN), 'W_l1': lin(ks[4], H, H), 'b_l1': jnp.zeros((H,), jnp.float32), 'W_r1': lin(ks[5], H, H), 'W_lin1': lin(ks[6], H, H), 'b_lin1': jnp.zeros((H,), jnp.float32), 'W_lin2': lin(ks[7], C, H), 'b_lin2': jnp.zeros((C,), jnp.float32)}
    _L1_gnn_all = _L1_gnn_setup()
    _L1_gnn_in = {k: v for k, v in _L1_gnn_all.items() if k in ('W_l0', 'b_l0', 'W_r0', 'W_l1', 'b_l1', 'W_r1', 'W_lin1', 'b_lin1', 'W_lin2', 'b_lin2')}
    del _L1_gnn_all
    return {'x': x, 'src': src, 'dst': dst, 'L0_gnn_W1': _L0_gnn_in['W1'], 'L0_gnn_b1': _L0_gnn_in['b1'], 'L0_gnn_W2': _L0_gnn_in['W2'], 'L0_gnn_b2': _L0_gnn_in['b2'], 'L1_gnn_W_l0': _L1_gnn_in['W_l0'], 'L1_gnn_b_l0': _L1_gnn_in['b_l0'], 'L1_gnn_W_r0': _L1_gnn_in['W_r0'], 'L1_gnn_W_l1': _L1_gnn_in['W_l1'], 'L1_gnn_b_l1': _L1_gnn_in['b_l1'], 'L1_gnn_W_r1': _L1_gnn_in['W_r1'], 'L1_gnn_W_lin1': _L1_gnn_in['W_lin1'], 'L1_gnn_b_lin1': _L1_gnn_in['b_lin1'], 'L1_gnn_W_lin2': _L1_gnn_in['W_lin2'], 'L1_gnn_b_lin2': _L1_gnn_in['b_lin2']}

def reference(x, src, dst, L0_gnn_W1, L0_gnn_b1, L0_gnn_W2, L0_gnn_b2, L1_gnn_W_l0, L1_gnn_b_l0, L1_gnn_W_r0, L1_gnn_W_l1, L1_gnn_b_l1, L1_gnn_W_r1, L1_gnn_W_lin1, L1_gnn_b_lin1, L1_gnn_W_lin2, L1_gnn_b_lin2):
    import jax
    import jax.numpy as jnp

    def _L0_gnn_ref(x, edge_src, edge_dst, W1, b1, W2, b2):
        import jax, jax.numpy as jnp
        import numpy as np
        N, E = (50000, 25000)
        D_IN, D_HID, D_OUT = (128, 256, 128)

        def _sage_layer(h, edge_src, edge_dst, W, b, inv_deg):
            msgs = h[edge_src]
            agg = jax.ops.segment_sum(msgs, edge_dst, num_segments=h.shape[0]) * inv_deg
            y = jnp.concatenate([h, agg], axis=1)
            return y @ W + b
        n = x.shape[0]
        deg = jax.ops.segment_sum(jnp.ones_like(edge_dst, dtype=x.dtype), edge_dst, num_segments=n)
        inv_deg = (1.0 / jnp.maximum(deg, 1.0))[:, None]
        h = _sage_layer(x, edge_src, edge_dst, W1, b1, inv_deg)
        h = jax.nn.relu(h)
        h = _sage_layer(h, edge_src, edge_dst, W2, b2, inv_deg)
        return jax.nn.log_softmax(h, axis=1)

    def _L1_gnn_ref(x, edge_index, W_l0, b_l0, W_r0, W_l1, b_l1, W_r1, W_lin1, b_lin1, W_lin2, b_lin2):
        import jax, jax.numpy as jnp
        import numpy as np

        def _sage_conv(x, src, dst, W_l, b_l, W_r, n_nodes):
            msgs = x[src]
            agg = jax.ops.segment_sum(msgs, dst, num_segments=n_nodes)
            deg = jax.ops.segment_sum(jnp.ones((src.shape[0],), x.dtype), dst, num_segments=n_nodes)
            mean = agg / jnp.clip(deg, 1.0)[:, None]
            return mean @ W_l.T + b_l + x @ W_r.T
        src, dst = (edge_index[0], edge_index[1])
        n = x.shape[0]
        h = jax.nn.relu(_sage_conv(x, src, dst, W_l0, b_l0, W_r0, n))
        h = jax.nn.relu(_sage_conv(h, src, dst, W_l1, b_l1, W_r1, n))
        h = jax.nn.relu(h @ W_lin1.T + b_lin1)
        return h @ W_lin2.T + b_lin2
    edge_index = jnp.stack([src, dst])
    h = jnp.maximum(_layernorm(x, axis=-1), 0.0)
    x = x + _L0_gnn_ref(h, src, dst, L0_gnn_W1, L0_gnn_b1, L0_gnn_W2, L0_gnn_b2)
    h = jnp.maximum(_layernorm(x, axis=-1), 0.0)
    x = x + _L1_gnn_ref(h, edge_index, L1_gnn_W_l0, L1_gnn_b_l0, L1_gnn_W_r0, L1_gnn_W_l1, L1_gnn_b_l1, L1_gnn_W_r1, L1_gnn_W_lin1, L1_gnn_b_lin1, L1_gnn_W_lin2, L1_gnn_b_lin2)
    return x

_drawn_inputs = setup_inputs


def setup_inputs(seed=0):
    import zlib

    import numpy as np

    out = dict(_drawn_inputs(seed))
    spreads = {'L1_gnn_b_l0': (0.0, 0.8),
     'L1_gnn_b_l1': (0.0, 0.8),
     'L1_gnn_b_lin1': (0.0, 0.591),
     'L1_gnn_b_lin2': (0.0, 0.401)}
    factors = {'L0_gnn_W1': 2.823, 'L0_gnn_b1': 8.0, 'L0_gnn_b2': 8.0}
    for name, (base, spread) in spreads.items():
        noise = np.random.default_rng([zlib.crc32(name.encode()), seed]).standard_normal(out[name].shape)
        drawn = base * np.exp(spread * noise) if base else spread * noise
        out[name] = jnp.asarray(drawn.astype(out[name].dtype))
    for name, factor in factors.items():
        out[name] = (out[name] * factor).astype(out[name].dtype)
    return out
```

```python
from contextlib import ExitStack

import concourse.bass as bass
from concourse import mybir

F32 = mybir.dt.float32
F16 = mybir.dt.float16
I32 = mybir.dt.int32
ALU = mybir.AluOpType
ACT = mybir.ActivationFunctionType
AX = mybir.AxisListType.X
ds = bass.ds

N = 3125
E = 50000
D = 128
H = 256
P = 125
S = N // P
ER = 125
EC = E // ER

WD = 5
NWIN = N // WD
KEY = 128
WKEY = WD * S * KEY
CAP = 128
GW = 4
QG = NWIN // P
DIV_M, DIV_S = 4195, 19

C = 500
NFULL = N // C
NCH = NFULL + 1
BANK = 512
NW = 14
HALVES = {True: ((0, 2), (2, 4)), False: ((0, 1),)}
LN_SCALE = 4096.0
LN_BOUND = 11.5
TOP = 32768.0
EXP_MASK = 0x7F800000
EXP_FLIP = 254 << 23


def width(full):
    return C if full else N - NFULL * C


def sage_program(nc, x, src, dst, W1, b1, W2, b2, Wl0, bl0, Wr0, Wl1, bl1, Wr1, Wa, ba, Wb, bb, out):
    ctx = ExitStack()
    with ctx:
        def sb(name, cols, dt=F32):
            return ctx.enter_context(nc.sbuf_tensor(name, [128, cols], dt))

        sems = {}

        def sem(name):
            if name not in sems:
                sems[name] = ctx.enter_context(nc.semaphore(name))
            return sems[name]

        def over(t, at, cols, dt):
            n = cols * (2 if dt == F16 else 4) // 2
            v = t[:, at // 2:at // 2 + n]
            return v if dt == F16 else v.bitcast(dt)

        key_d = nc.dram_tensor("key_d", [E + ER * 2], F32, kind="Internal").ap()
        inv_d = nc.dram_tensor("inv_d", [N], F32, kind="Internal").ap()
        wt_d = nc.dram_tensor("wt_d", [128, 2304], F32, kind="Internal").ap()
        self_d = nc.dram_tensor("self_d", [128, N], F32, kind="Internal").ap()
        x1_d = nc.dram_tensor("x1_d", [N, D], F32, kind="Internal").ap()
        hs_d1 = nc.dram_tensor("hs_d1", [N, 2 * D], F16, kind="Internal").ap()
        hs_d2 = nc.dram_tensor("hs_d2", [N, 2 * D], F16, kind="Internal").ap()
        hs_d3 = nc.dram_tensor("hs_d3", [N, 2 * D], F16, kind="Internal").ap()
        hs_d4 = nc.dram_tensor("hs_d4", [N, 2 * H], F16, kind="Internal").ap()

        adj = sb("adj", S * N + 1, F16)
        hs_a = sb("hs_a", S * 2 * D, F16)
        hs_b = sb("hs_b", S * 2 * H, F16)
        wts = sb("wts", 1024)
        invc = sb("invc", C)
        aggT = sb("aggT", 2 * C)
        actT = sb("actT", 2 * C)
        zT = sb("zT", C)
        identf = sb("identf", 128)
        identh = sb("identh", 128, F16)
        st = sb("st", 64)
        col = sb("col", 40)
        ps = ctx.enter_context(nc.psum_tensor("ps", [128, 8 * BANK], F32))

        def bank(i, cols=BANK, rows=128):
            return ps[0:rows, i * BANK:i * BANK + cols]

        b1c, b2c, bl0c, bl1c, bac, bbc = (col[:, 0:2], col[:, 2:3], col[:, 3:5], col[:, 5:7], col[:, 7:9], col[:, 9:10])
        s3, is3, b3s = col[:, 10:12], col[:, 12:14], col[:, 14:16]
        zs, izs = col[:, 16:17], col[:, 17:18]
        bnd = col[:, 18:20]
        tmp2 = col[:, 20:22]
        epsc = col[:, 22:23]
        ones_c = col[:, 23:24]
        flag_f = col[:, 24:25]
        flag_i = col[:, 25:26].bitcast(I32)
        bndz = col[:, 26:27]
        tmp3 = col[:, 28:30]

        o = [0]

        def lay(cols, dt):
            at = o[0]
            o[0] += (cols * (2 if dt == F16 else 4) + 63) // 64 * 64
            return over(adj, at, cols, dt)
        dst_i, src_i, t_i, s_i = (lay(EC, I32)[0:ER] for _ in range(4))
        dstf, keyf, dstrel = (lay(EC, F32)[0:ER] for _ in range(3))
        rows = lay(QG * EC, F32)[0:P]
        gk = lay(QG * CAP, F32)[0:P]
        scr = lay(2 * H * QG, F32)
        xs0, xc0, sq0 = (lay(S * D, F32)[0:P] for _ in range(3))
        wn = lay(2304, F32)
        wt_s = lay(2304, F32)
        thr = lay(QG, F32)[0:P]
        wbase = lay(QG, F32)[0:P]
        cnt = lay(8 * QG, F32)[0:P]
        rowi = lay(QG, I32)[0:P]
        rowf = lay(QG, F32)[0:P]
        starti = lay(QG, I32)[0:P]
        diag = lay(ER, F32)[0:ER]
        onesf = lay(128, F32)
        deg = lay(QG * WD, F32)[0:P]
        st0 = lay(S * 4, F32)[0:P]
        k_i = lay(NWIN, I32)
        kp_i = lay(NWIN, I32)
        padk = lay(256, F32)
        iota5 = lay(C, F16)[0:ER]
        zeros = lay(C, F16)[0:ER]
        onesh = lay(128, F16)[0:ER]
        oh = lay(C, F16)[0:ER]
        gbuf = lay(2 * H, F16)[0:ER]
        idx = lay(1, I32)[0:ER]
        assert o[0] <= S * N * 2
        up = S * 2 * D * 2
        kp = over(hs_b, up, NWIN, F32)
        kn = over(hs_b, up + 2560, NWIN, F32)
        ohp = [over(hs_b, up + 5120 + 1024 * i, GW * 128, F16) for i in range(2)]
        ohn = [over(hs_b, up + 7168 + 1024 * i, GW * 128, F16) for i in range(2)]
        iota_h = over(hs_b, up + 9216, 128, F16)
        selfT = over(hs_b, up + 9472, C, F32)
        xin, yc, sqb, x1b, hb = (over(hs_b, up + 2048 * i, 4 * D, F32)[0:P] for i in range(5))
        selfc = over(hs_b, up + 10240, C, F32)
        w4 = over(hs_a, 0, 1792, F32)
        x1in = over(hs_a, 7168, 4 * D, F32)[0:P]
        outb = over(hs_a, 9216, 4 * D, F32)[0:P]

        w1v = wts[:, 0:512].rearrange("p (k o) -> p k o", k=2)
        w2v = wts[:, 512:1024].rearrange("p (k o) -> p k o", k=4)
        ha = hs_a[0:P]
        hbz = hs_b[0:P]

        def tiles(t, w):
            return t.rearrange("p (t d) -> p t d", d=w)

        def absolute(o, v):
            return nc.vector.tensor_scalar(o.bitcast(I32), v.bitcast(I32), 0x7FFFFFFF, None, ALU.bitwise_and)

        def hs_write(h, c, full, part, w):
            n = width(full) // P
            v = h[:, ds(c * (4 * 2 * w), n * 2 * w)].rearrange("p (t k d) -> p t k d", k=2, d=w)
            return v[:, :, part, :]

        class Link:

            def __init__(self, eng, name, base=0):
                self.eng, self.sem, self.base, self.n = eng, sem(name), base, 0

            def __call__(self, ins):
                self.n += 1
                ins.then_inc(self.sem, 1)
                self.eng.wait_ge(self.sem, self.base + self.n)

        def wait_past(eng, name, value):
            if not isinstance(value, int) or value > 0:
                eng.wait_ge(sem(name), value)

        def chunks(eng, emit):
            emit(0, True)
            with eng.Fori(1, NFULL) as c:
                emit(c, True)
            emit(NFULL, False)

        def ln_dve(dve, lk, p, k, X, XC, SQ, stat, T, hi, lo, before=None):
            m, v = stat[:, 0:T], stat[:, T:2 * T]
            bc = lambda a: a.unsqueeze(2).to_broadcast([P, T, D])
            X3, XC3, SQ3 = (tiles(t, D) for t in (X, XC, SQ))
            lk(nc.vector.tensor_reduce(m, X3, AX, ALU.add))
            lk(nc.vector.tensor_scalar(m, m, 1.0 / D, None, ALU.mult))
            nc.vector.tensor_tensor(XC3, X3, bc(m), ALU.subtract).then_inc(sem(p + "centred"), 1)
            if before:
                before()
            dve.wait_ge(sem(p + "squares"), k)
            nc.vector.tensor_reduce(v, SQ3, AX, ALU.add).then_inc(sem(p + "sumsq"), 1)
            dve.wait_ge(sem(p + "std"), k)
            lk(nc.vector.reciprocal(v, v))
            lk(nc.vector.tensor_scalar(v, v, LN_SCALE, None, ALU.mult))
            dve.wait_ge(sem(p + "centred"), k)
            nc.vector.tensor_tensor(SQ3, XC3, bc(v), ALU.mult).then_inc(sem(p + "normed"), 1)
            dve.wait_ge(sem(p + "high"), k)
            nc.vector.scalar_tensor_tensor(lo, SQ3, 0.0, hi, ALU.max, ALU.subtract).then_inc(sem(p + "low"), 1)

        def ln_act(act, p, k, XC, SQ, stat, T, hi):
            v = stat[:, T:2 * T]
            act.wait_ge(sem(p + "centred"), k)
            nc.scalar.activation(SQ, XC, ACT.Square).then_inc(sem(p + "squares"), 1)
            act.wait_ge(sem(p + "sumsq"), k)
            nc.scalar.activation(v, v, ACT.Sqrt, bias=epsc[0:P], scale=1.0 / D).then_inc(sem(p + "std"), 1)
            act.wait_ge(sem(p + "normed"), k)
            nc.scalar.activation(hi, tiles(SQ, D), ACT.Relu).then_inc(sem(p + "high"), 1)

        block = ctx.enter_context(nc.Block())

        h0v = ha.rearrange("p (t k d) -> p t k d", k=2, d=D)
        WN = {"l0": (0, 1, 2), "r0": (256, 1, 2), "l1": (512, 2, 2), "r1": (1024, 2, 2), "a": (1536, 2, 2), "b": (2048, 2, 1)}

        def sp_layers(sp, slow):
            if not slow:
                sp.wait_ge(sem("inverse"), 1)
                with nc.allow_non_contiguous_dma(reason="runs of 5 inverse degrees"):
                    sp.dma_start(inv_d.rearrange("(g q j) -> q g j", q=P, j=WD),
                                 deg.rearrange("q (g j) -> q g j", j=WD)).then_inc(sem("inv_out"), 16)
            else:
                def store_inv(c, full):
                    sp.wait_ge(sem("sd_inv"), c + 1)
                    sp.dma_start(inv_d[ds(c * C, width(full))].rearrange("(o e) -> o e", o=1),
                                 invc[0:1, 0:width(full)]).then_inc(sem("inv_out"), 16)
                    sp.wait_ge(sem("inv_out"), 16 * c + 16)
                    sp.sem_inc(sem("inv_out_seen"), 1)
                chunks(sp, store_inv)
            ninv = NCH if slow else 1
            sp.wait_ge(sem("inv_out"), 16 * ninv)

            def load_inv(p, c, full):
                sp.dma_start(invc[:, 0:width(full)],
                             inv_d[ds(c * C, width(full))].partition_broadcast(128)).then_inc(sem(p + "inv"), 16)

            def spread(ph, hs, w, hd):
                if slow:
                    sp.dma_start(hd.rearrange("(t p) f -> p t f", p=P),
                                 hs.rearrange("p (t f) -> p t f", f=2 * w)).then_inc(sem(f"p{ph}_rows"), 16)

            def each(emit):
                emit(0, True, True)
                with sp.Fori(1, NFULL - 1) as c:
                    emit(c, True, True)
                emit(NFULL - 1, True, False)
                emit(NFULL, False, None)

            sp.wait_ge(sem("n_low"), 1)
            spread(1, ha, D, hs_d1)
            load_inv("p1_", 0, True)

            def step1(c, full, nxt):
                sp.wait_ge(sem("p1_agg_out"), c + 1)
                if nxt is not None:
                    load_inv("p1_", c + 1, nxt)
                sp.wait_ge(sem("p1_self"), c + 1)
                sp.dma_start(self_d[:, ds(c * C, width(full))], selfT[:, 0:width(full)]).then_inc(sem("p1_self_out"), 16)
            each(step1)
            sp.wait_ge(sem("p1_h1"), 2 * NCH)
            sp.wait_ge(sem("wt_out"), 16)
            sp.dma_start(wts[:, 0:512], wt_d[:, 0:512]).then_inc(sem("w0_in"), 16)
            sp.wait_ge(sem("p1_self_out"), 16 * NCH)
            sp.wait_ge(sem("p1_low"), NCH)
            spread(2, hbz[:, 0:S * 2 * D], D, hs_d2)

            def load_self(c, full):
                sp.dma_start(selfc[:, 0:width(full)], self_d[:, ds(c * C, width(full))]).then_inc(sem("p2_self"), 16)

            def load_x(c, full):
                sp.dma_start(tiles(xin[:, 0:width(full) // P * D], D),
                             x[ds(c * C, width(full)), :].rearrange("(t p) d -> p t d", p=P)).then_inc(sem("p2_x"), 16)
            load_inv("p2_", 0, True)
            load_self(0, True)
            load_x(0, True)

            def step2(c, full, nxt):
                if nxt is not None:
                    sp.wait_ge(sem("p2_agg_out"), c + 1)
                    load_inv("p2_", c + 1, nxt)
                    sp.wait_ge(sem("p2_sum"), c + 1)
                    load_self(c + 1, nxt)
                    sp.wait_ge(sem("p2_x_used"), c + 1)
                    load_x(c + 1, nxt)
                sp.wait_ge(sem("p2_x1"), c + 1)
                sp.dma_start(x1_d[ds(c * C, width(full)), :].rearrange("(t p) d -> p t d", p=P),
                             tiles(x1b[:, 0:width(full) // P * D], D)).then_inc(sem("p2_x1_out"), 16)
            each(step2)
            sp.wait_ge(sem("p2_x1_out"), 16 * NCH)
            sp.wait_ge(sem("p2_low"), NCH)
            spread(3, ha, D, hs_d3)
            load_inv("p3_", 0, True)

            def step3(c, full, nxt):
                if nxt is not None:
                    sp.wait_ge(sem("p3_agg_out"), c + 1)
                    load_inv("p3_", c + 1, nxt)
            each(step3)
            sp.wait_ge(sem("p3_agg_out"), NCH)
            sp.wait_ge(sem("p3_own"), NCH)
            if slow:
                sp.wait_ge(sem("p3_rows"), 16)
            sp.dma_start(w4, wt_d[:, 512:2304]).then_inc(sem("w4_in"), 16)
            sp.wait_ge(sem("p3_low"), 2 * NCH - 1)
            spread(4, hbz, H, hs_d4)
            load_inv("p4_", 0, True)

            def load_x1(c, full):
                sp.dma_start(tiles(x1in[:, 0:width(full) // P * D], D),
                             x1_d[ds(c * C, width(full)), :].rearrange("(t p) d -> p t d", p=P)).then_inc(sem("p4_x1"), 16)
            load_x1(0, True)

            def step4(c, full, nxt):
                sp.wait_ge(sem("p4_agg_out"), 2 * c + 2)
                if nxt is not None:
                    load_inv("p4_", c + 1, nxt)
                sp.wait_ge(sem("p4_sum"), c + 1)
                sp.dma_start(out[ds(c * C, width(full)), :].rearrange("(t p) d -> p t d", p=P),
                             tiles(outb[:, 0:width(full) // P * D], D)).then_inc(sem("p4_out"), 16)
                if nxt is not None:
                    load_x1(c + 1, nxt)
            each(step4)
            sp.wait_ge(sem("p4_out"), 16 * NCH)

        def branch(eng, layers):
            eng.wait_ge(sem("flag"), 1)
            fits = eng.value_load(flag_i[0:1, 0:1], min_val=0, max_val=1)
            with eng.If(fits == 1):
                layers(eng, False)
            with eng.Else():
                layers(eng, True)

        def pool_layers(pool, slow):
            if not slow:
                return
            nc.gpsimd.iota(iota5, [[1, C]], base=0, channel_multiplier=0,
                           allow_small_or_imprecise_dtypes=True).then_inc(sem("slow_consts"), 1)
            nc.gpsimd.memset(zeros, 0.0).then_inc(sem("slow_consts"), 1)
            nc.gpsimd.memset(onesh, 1.0).then_inc(sem("slow_consts"), 1)
            for ph, hd, w in ((1, hs_d1, D), (2, hs_d2, D), (3, hs_d3, D), (4, hs_d4, H)):
                pool.wait_ge(sem(f"p{ph}_rows"), 16)
                with pool.Fori(0, NCH * EC) as u:
                    pool.wait_ge(sem(f"p{ph}_edge"), 2 * u + 2)
                    pool.sem_inc(sem(f"p{ph}_edge_seen"), 1)
                    pool.indirect_dma_start(gbuf[:, 0:2 * w], None, hd,
                                            bass.IndirectOffsetOnAxis(idx, 0)).then_inc(sem(f"p{ph}_gathered"), 16)

        def dve_slow(dve, ph, c):
            with dve.Fori(0, EC) as j:
                u = c * EC + j
                dve.wait_ge(sem(f"p{ph}_edge_used"), u + 1)
                nc.vector.tensor_copy(idx, src_i[:, ds(j, 1)]).then_inc(sem(f"p{ph}_edge"), 1)
                nc.vector.tensor_scalar(oh, iota5, dstrel[:, ds(j, 1)], None, ALU.is_equal).then_inc(sem(f"p{ph}_edge"), 1)
            Link(dve, f"dve_slow{ph}", c)(nc.vector.tensor_scalar(dstrel, dstrel, float(-C), None, ALU.add))

        def pe_slow(pe, ph, c, full, accs, w):
            n = width(full)
            for a in accs:
                nc.tensor.matmul(a, zeros[:, 0:128], zeros[:, 0:n], start=True, stop=False, skip_group_check=True)
            with pe.Fori(0, EC) as j:
                u = c * EC + j
                pe.wait_ge(sem(f"p{ph}_edge"), 2 * u + 2)
                if w:
                    pe.wait_ge(sem(f"p{ph}_gathered"), 16 * u + 16)
                for h, a in enumerate(accs):
                    for part in range(2 if w else 1):
                        lhs = gbuf[:, part * w + h * 128:part * w + h * 128 + 128] if w else onesh
                        last = nc.tensor.matmul(a, lhs, oh[:, 0:n], start=False, stop=False, skip_group_check=True)
                last.then_inc(sem(f"p{ph}_edge_used"), 1)
            for a in accs:
                last = nc.tensor.matmul(a, zeros[:, 0:128], zeros[:, 0:n], start=False, stop=True, skip_group_check=True)
            return last

        def dve_layers(dve, slow):
            if slow:
                dve.wait_ge(sem("slow_consts"), 3)
                dve.sem_inc(sem("p0_edge_used"), 1)
                Link(dve, "dve_s0")(nc.vector.tensor_copy(dstrel, dstf))

                def degrees(c, full):
                    n = width(full)
                    lk = Link(dve, "dve_s1", c)
                    dve_slow(dve, 0, c)
                    dve.wait_ge(sem("p0_agg"), c + 1)
                    wait_past(dve, "inv_out", 16 * c)
                    lk(nc.vector.tensor_scalar(invc[:, 0:n], bank(2, n), 1.0, None, ALU.max))
                    nc.vector.reciprocal(invc[:, 0:n], invc[:, 0:n]).then_inc(sem("sd_inv"), 1)
                chunks(dve, degrees)

            def slow_reset(ph):
                if slow:
                    dve.sem_inc(sem(f"p{ph}_edge_used"), 1)
                    Link(dve, f"dve_s{ph + 1}")(nc.vector.tensor_copy(dstrel, dstf))

            def build(c, full):
                nw = GW if full else 1

                def group(g, k, wait):
                    wait_past(dve, "counted", wait)
                    for w in range(nw):
                        win = g * GW + w if full else NFULL * S * GW + (g - NFULL * S)
                        nc.vector.tensor_scalar(ohp[k][:, w * 128:(w + 1) * 128], iota_h, kp[:, ds(win, 1)], None, ALU.is_equal)
                        last = nc.vector.tensor_scalar(ohn[k][:, w * 125:(w + 1) * 125], iota_h[:, 0:125], kn[:, ds(win, 1)],
                                                       None, ALU.is_equal)
                    last.then_inc(sem("onehot"), 1)
                group(c * S, 0, c * S)
                for i in (1, 2):
                    group(c * S + i, i % 2, c * S + i - 1)
                with dve.Fori(1, (S - 1) // 2) as h:
                    group(c * S + 1 + 2 * h, 1, c * S + 2 * h)
                    group(c * S + 2 + 2 * h, 0, c * S + 1 + 2 * h)

            def step1(c, full, nxt):
                n = width(full)
                if nxt is not None and not slow:
                    build(c + 1, nxt)
                if slow:
                    dve_slow(dve, 1, c)
                dve.wait_ge(sem("p1_inv"), 16 * c + 16)
                dve.wait_ge(sem("p1_agg"), c + 1)
                wait_past(dve, "p1_h1", 2 * c)
                nc.vector.tensor_tensor(aggT[:, 0:n], bank(2, n), invc[:, 0:n], ALU.mult).then_inc(sem("p1_agg_out"), 1)
                dve.wait_ge(sem("p1_selfs"), c + 1)
                wait_past(dve, "p1_self_out", 16 * c)
                nc.vector.tensor_scalar(selfT[:, 0:n], bank(7, n), b2c, None, ALU.add).then_inc(sem("p1_self"), 1)
                dve.wait_ge(sem("p1_high"), c + 1)
                nt = n // P
                nc.vector.tensor_tensor(hs_write(hbz, c, full, 1, D), tiles(bank(3, nt * D, P), D),
                                        hs_write(hbz, c, full, 0, D), ALU.subtract).then_inc(sem("p1_low"), 1)

            def each(emit):
                emit(0, True, True)
                with dve.Fori(1, NFULL - 1) as c:
                    emit(c, True, True)
                emit(NFULL - 1, True, False)
                emit(NFULL, False, None)
            slow_reset(1)
            if not slow:
                build(0, True)
            each(step1)

            slow_reset(2)
            dve.wait_ge(sem("p1_self_out"), 16 * NCH)

            def step2(c, full):
                n = width(full)
                nt = n // P
                K2 = 5
                lk = Link(dve, "dve2", K2 * c)
                if slow:
                    dve_slow(dve, 2, c)
                o2 = aggT[:, 0:n]
                dve.wait_ge(sem("p2_inv"), 16 * c + 16)
                dve.wait_ge(sem("p2_agg"), c + 1)
                wait_past(dve, "p2_turned", c)
                nc.vector.scalar_tensor_tensor(o2, bank(2, n), izs, invc[:, 0:n], ALU.mult, ALU.mult).then_inc(sem("p2_agg_out"), 1)
                dve.wait_ge(sem("p2_agg_out"), c + 1)
                dve.wait_ge(sem("p2_self"), 16 * c + 16)
                nc.vector.tensor_tensor(o2, o2, selfc[:, 0:n], ALU.add).then_inc(sem("p2_sum"), 1)
                bc = lambda a: a.unsqueeze(2).to_broadcast([P, nt, D])
                v = lambda t: tiles(t[:, 0:nt * D], D)
                m, sm, ls = st[0:P, 8:8 + nt], st[0:P, 12:12 + nt], st[0:P, 16:16 + nt]
                y = tiles(bank(3, nt * D, P), D)
                dve.wait_ge(sem("p2_turned"), c + 1)
                lk(nc.vector.tensor_reduce(m, y, AX, ALU.max))
                nc.vector.tensor_tensor(v(yc), y, bc(m), ALU.subtract).then_inc(sem("p2_shifted"), 1)
                dve.wait_ge(sem("p2_shifted"), c + 1)
                dve.wait_ge(sem("p2_x"), 16 * c + 16)
                wait_past(dve, "p2_x1_out", 16 * c)
                nc.vector.tensor_tensor(v(x1b), v(xin), v(yc), ALU.add).then_inc(sem("p2_x_used"), 1)
                dve.wait_ge(sem("p2_exp"), c + 1)
                nc.vector.tensor_reduce(sm, v(sqb), AX, ALU.add).then_inc(sem("p2_expsum"), 1)
                dve.wait_ge(sem("p2_lse"), c + 1)
                dve.wait_ge(sem("p2_x_used"), c + 1)
                nc.vector.tensor_tensor(v(x1b), v(x1b), bc(ls), ALU.subtract).then_inc(sem("p2_x1"), 1)
                dve.wait_ge(sem("p2_x1"), c + 1)
                ln_dve(dve, lk, "p2_", c + 1, x1b[:, 0:nt * D], yc[:, 0:nt * D], sqb[:, 0:nt * D], st[0:P],
                       nt, hs_write(ha, c, full, 0, D), hs_write(ha, c, full, 1, D))
                assert lk.n == K2
            chunks(dve, step2)

            slow_reset(3)
            dve.wait_ge(sem("p2_x1_out"), 16 * NCH)

            def step3(c, full):
                n = width(full)
                nt = n // P
                if slow:
                    dve_slow(dve, 3, c)
                dve.wait_ge(sem("p3_inv"), 16 * c + 16)
                dve.wait_ge(sem("p3_agg"), c + 1)
                wait_past(dve, "p3_h3", 2 * c)
                nc.vector.tensor_tensor(aggT[:, 0:n], bank(2, n), invc[:, 0:n], ALU.mult).then_inc(sem("p3_agg_out"), 1)
                for k, (t0, t1) in enumerate(HALVES[full]):
                    dve.wait_ge(sem("p3_high"), 2 * c + k + 1)
                    nc.vector.tensor_tensor(hs_write(hbz, c, full, 1, H)[:, t0:t1], tiles(bank(6 + k, (t1 - t0) * H, P), H),
                                            hs_write(hbz, c, full, 0, H)[:, t0:t1], ALU.subtract).then_inc(sem("p3_low"), 1)
            chunks(dve, step3)

            slow_reset(4)

            def step4(c, full):
                n = width(full)
                nt = n // P
                if slow:
                    dve_slow(dve, 4, c)
                dve.wait_ge(sem("p4_inv"), 16 * c + 16)
                wait_past(dve, "p4_lin2", c)
                for h in range(2):
                    dve.wait_ge(sem("p4_agg"), 2 * c + h + 1)
                    nc.vector.tensor_tensor(aggT[:, h * C:h * C + n], bank(h, n), invc[:, 0:n], ALU.mult).then_inc(sem("p4_agg_out"), 1)
                dve.wait_ge(sem("p4_turned"), c + 1)
                dve.wait_ge(sem("p4_x1"), 16 * c + 16)
                wait_past(dve, "p4_out", 16 * c)
                nc.vector.tensor_tensor(outb[:, 0:nt * D], bank(3, nt * D, P), x1in[:, 0:nt * D], ALU.add).then_inc(sem("p4_sum"), 1)
            chunks(dve, step4)

        def act_layers(act, slow):
            def build(c, full):
                nd = C // S if full else WD

                def group(g, k):
                    act.wait_ge(sem("counted"), g + 1)
                    at = g * (C // S) if full else NFULL * C + (g - NFULL * S) * WD
                    v = adj[0:P, 0:S * N].rearrange("p (t n) -> p t n", n=N)
                    nc.scalar.activation(v[:, :, ds(at, nd)], bank(k, nd * S, P).rearrange("p (d t) -> p t d", t=S),
                                         ACT.Copy).then_inc(sem("evicted"), 1)
                group(c * S, 0)
                with act.Fori(0, (S - 1) // 2) as h:
                    group(c * S + 1 + 2 * h, 1)
                    group(c * S + 2 + 2 * h, 0)

            def step1(c, full, nxt):
                n = width(full)
                nt = n // P
                if nxt is not None and not slow:
                    build(c + 1, nxt)
                act.wait_ge(sem("p1_own"), c + 1)
                wait_past(act, "p1_h1", 2 * c)
                nc.scalar.activation(aggT[:, C:C + n], bank(3, n), ACT.Copy).then_inc(sem("p1_h0T"), 1)
                wait_past(act, "p1_selfs", c)
                for m in range(2):
                    act.wait_ge(sem("p1_h1"), 2 * c + m + 1)
                    nc.scalar.activation(actT[:, m * C:m * C + n], bank(4 + m, n), ACT.Relu, bias=b1c[:, m:m + 1]).then_inc(sem("p1_relu"), 1)
                act.wait_ge(sem("p1_zm"), c + 1)
                wait_past(act, "p1_turned", c)
                nc.scalar.activation(zT[:, 0:n], bank(6, n), ACT.Identity, scale=zs).then_inc(sem("p1_zT"), 1)
                act.wait_ge(sem("p1_turned"), c + 1)
                nc.scalar.activation(hs_write(hbz, c, full, 0, D), tiles(bank(3, nt * D, P), D), ACT.Copy).then_inc(sem("p1_high"), 1)

            def each(emit):
                emit(0, True, True)
                with act.Fori(1, NFULL - 1) as c:
                    emit(c, True, True)
                emit(NFULL - 1, True, False)
                emit(NFULL, False, None)
            if not slow:
                act.wait_ge(sem("n_low"), 1)
                act.wait_ge(sem("wt_out"), 16)
                act.wait_ge(sem("inv_out"), 16)
                act.wait_ge(sem("onehot"), 1)
                build(0, True)
            each(step1)

            def step2(c, full):
                nt = width(full) // P
                v = lambda t: t[:, 0:nt * D]
                act.wait_ge(sem("p2_shifted"), c + 1)
                nc.scalar.activation(v(sqb), v(yc), ACT.Exp).then_inc(sem("p2_exp"), 1)
                act.wait_ge(sem("p2_expsum"), c + 1)
                nc.scalar.activation(st[0:P, 16:16 + nt], st[0:P, 12:12 + nt], ACT.Ln).then_inc(sem("p2_lse"), 1)
                ln_act(act, "p2_", c + 1, v(yc), v(sqb), st[0:P], nt, hs_write(ha, c, full, 0, D))
            chunks(act, step2)

            act.wait_ge(sem("p2_x1_out"), 16 * NCH)

            def step3(c, full):
                n = width(full)
                nt = n // P
                act.wait_ge(sem("p3_own"), c + 1)
                wait_past(act, "p3_h3", 2 * c)
                nc.scalar.activation(aggT[:, C:C + n], bank(3, n), ACT.Copy).then_inc(sem("p3_ownT"), 1)
                wait_past(act, "p3_turned", 2 * c)
                for m in range(2):
                    act.wait_ge(sem("p3_h3"), 2 * c + m + 1)
                    nc.scalar.activation(actT[:, m * C:m * C + n], bank(4 + m, n), ACT.Relu, bias=b3s[:, m:m + 1],
                                         scale=s3[:, m:m + 1]).then_inc(sem("p3_relu"), 1)
                for k, (t0, t1) in enumerate(HALVES[full]):
                    act.wait_ge(sem("p3_turned"), 2 * c + k + 1)
                    nc.scalar.activation(hs_write(hbz, c, full, 0, H)[:, t0:t1], tiles(bank(6 + k, (t1 - t0) * H, P), H),
                                         ACT.Copy).then_inc(sem("p3_high"), 1)
            chunks(act, step3)

            h3T = wts[:, 0:2 * C]

            def step4(c, full):
                n = width(full)
                for m in range(2):
                    act.wait_ge(sem("p4_own"), 2 * c + m + 1)
                    if m == 0:
                        wait_past(act, "p4_turned", c)
                    nc.scalar.activation(h3T[:, m * C:m * C + n], bank(2 + m, n), ACT.Copy).then_inc(sem("p4_ownT"), 1)
                for m in range(2):
                    act.wait_ge(sem("p4_h4"), 2 * c + m + 1)
                    nc.scalar.activation(actT[:, m * C:m * C + n], bank(4 + m, n), ACT.Relu, bias=bl1c[:, m:m + 1]).then_inc(sem("p4_relu"), 1)
                for m in range(2):
                    act.wait_ge(sem("p4_lin1"), 2 * c + m + 1)
                    nc.scalar.activation(aggT[:, m * C:m * C + n], bank(6 + m, n), ACT.Relu, bias=bac[:, m:m + 1]).then_inc(sem("p4_relu2"), 1)
                act.wait_ge(sem("p4_lin2"), c + 1)
                nc.scalar.activation(h3T[:, 0:n], bank(2, n), ACT.Identity, bias=bbc).then_inc(sem("p4_lin2T"), 1)
            chunks(act, step4)

        def pe_layers(pe, slow):
            def aggregate(acc, hs, w, h, c, full, s):
                n = width(full)
                for part in range(2):
                    last = nc.tensor.matmul(acc[:, 0:n], hs[:, ds(s * (2 * w) + part * w + h * 128, 128)],
                                            adj[0:P, ds(s * N + c * C, n)],
                                            start=(isinstance(s, int) and s == 0 and part == 0),
                                            stop=(isinstance(s, int) and s == S - 1 and part == 1), skip_group_check=True)
                return last

            def own(hs, w, h, b, c, full):
                for t in range(width(full) // P):
                    for part in range(2):
                        last = nc.tensor.matmul(bank(b)[:, t * P:(t + 1) * P],
                                                hs[:, ds((c * 4 + t) * (2 * w) + part * w + h * 128, 128)],
                                                identh[0:P, 0:P], start=(part == 0), stop=(part == 1))
                return last

            def dense(b, n, terms):
                for k, (wt, v) in enumerate(terms):
                    last = nc.tensor.matmul(bank(b, n), wt, v, start=(k == 0), stop=(k == len(terms) - 1))
                return last

            if slow:
                pe.wait_ge(sem("slow_consts"), 3)

                def degrees(c, full):
                    wait_past(pe, "sd_inv", c)
                    pe_slow(pe, 0, c, full, [bank(2, width(full))], 0).then_inc(sem("p0_agg"), 1)
                chunks(pe, degrees)

            def count(g, k, c_full, wait):
                pe.wait_ge(sem("onehot"), g + 1)
                wait_past(pe, "evicted", wait)
                for w in range(GW if c_full else 1):
                    last = nc.tensor.matmul(bank(k)[:, w * 125:(w + 1) * 125], ohp[k][:, w * 128:(w + 1) * 128],
                                            ohn[k][:, w * 125:(w + 1) * 125], start=True, stop=True)
                last.then_inc(sem("counted"), 1)

            def step1(c, full, nxt):
                n = width(full)
                nt = n // P
                acc = bank(2)
                wait_past(pe, "p1_agg_out", c)
                if slow:
                    pe_slow(pe, 1, c, full, [acc[:, 0:n]], D).then_inc(sem("p1_agg"), 1)
                elif nxt is not None:
                    g = (c + 1) * S
                    pe.wait_ge(sem("evicted"), g)
                    count(g, 0, nxt, g)
                    aggregate(acc, ha, D, 0, c, full, 0)
                    with pe.Fori(0, (S - 1) // 2 - 1) as h:
                        for k in (1, 2):
                            count(g + 2 * h + k, k % 2, nxt, g + 2 * h + k - 1)
                            aggregate(acc, ha, D, 0, c, full, 2 * h + k)
                    for i in (S - 2, S - 1):
                        count(g + i, i % 2, nxt, g + i - 1)
                        last = aggregate(acc, ha, D, 0, c, full, i)
                    last.then_inc(sem("p1_agg"), 1)
                else:
                    pe.wait_ge(sem("evicted"), NCH * S)
                    for s in range(S):
                        last = aggregate(acc, ha, D, 0, c, full, s)
                    last.then_inc(sem("p1_agg"), 1)
                wait_past(pe, "p1_low", c)
                own(ha, D, 0, 3, c, full).then_inc(sem("p1_own"), 1)
                wait_past(pe, "p1_relu", 2 * c)
                pe.wait_ge(sem("p1_h0T"), c + 1)
                pe.wait_ge(sem("p1_agg_out"), c + 1)
                for m in range(2):
                    dense(4 + m, n, [(w1v[:, 0, m * 128:m * 128 + 128], aggT[:, C:C + n]),
                                     (w1v[:, 1, m * 128:m * 128 + 128], aggT[:, 0:n])]).then_inc(sem("p1_h1"), 1)
                pe.wait_ge(sem("p1_relu"), 2 * c + 2)
                wait_past(pe, "p1_zT", c)
                dense(6, n, [(w2v[:, 2 + m, :], actT[:, m * C:m * C + n]) for m in range(2)]).then_inc(sem("p1_zm"), 1)
                wait_past(pe, "p1_self", c)
                dense(7, n, [(w2v[:, m, :], actT[:, m * C:m * C + n]) for m in range(2)]).then_inc(sem("p1_selfs"), 1)
                pe.wait_ge(sem("p1_zT"), c + 1)
                for t in range(nt):
                    last = nc.tensor.transpose(bank(3, 4 * D, P)[:, t * D:(t + 1) * D], zT[:, t * P:(t + 1) * P], identf[:])
                last.then_inc(sem("p1_turned"), 1)

            def each(emit):
                emit(0, True, True)
                with pe.Fori(1, NFULL - 1) as c:
                    emit(c, True, True)
                emit(NFULL - 1, True, False)
                emit(NFULL, False, None)
            pe.wait_ge(sem("n_low"), 1)
            pe.wait_ge(sem("w1_scaled"), 1)
            if slow:
                pe.wait_ge(sem("p1_rows"), 16)
            else:
                for i in range(3):
                    count(i, i % 2, True, i - 1)
                with pe.Fori(1, (S - 1) // 2) as h:
                    for k in (1, 2):
                        count(2 * h + k, k % 2, True, 2 * h + k - 1)
            each(step1)

            def staged(ph, agg_waits, aggs, parts):
                def step(c, full, before):
                    cut = [0, 7, 13, 19, S]
                    parts[0](c - 1, before) if before is not None else None
                    wait_past(pe, f"p{ph}_agg_out", len(aggs) * c)
                    todo = []
                    if slow:
                        w = aggs[0][2]
                        last = pe_slow(pe, ph, c, full, [a[0][:, 0:width(full)] for a in aggs], w)
                        last.then_inc(sem(f"p{ph}_agg"), len(aggs))
                        if before is not None:
                            for p in parts[1:]:
                                p(c - 1, before)
                        return
                    pieces = [(h, s) for h in range(len(aggs)) for s in range(S)]
                    npart = len(parts)
                    ends = [len(pieces) * (k + 1) // npart for k in range(npart)]
                    at = 0
                    for k in range(npart):
                        for h, s in pieces[at:ends[k]]:
                            acc, hs, w, hh = aggs[h]
                            last = aggregate(acc, hs, w, hh, c, full, s)
                            if s == S - 1:
                                last.then_inc(sem(f"p{ph}_agg"), 1)
                        at = ends[k]
                        if before is not None and k + 1 < npart:
                            parts[k + 1](c - 1, before)
                step(0, True, None)
                with pe.Fori(1, NFULL) as c:
                    step(c, True, True)
                step(NFULL, False, True)
                for p in parts:
                    p(NFULL, False)

            pe.wait_ge(sem("p1_low"), NCH)
            if slow:
                pe.wait_ge(sem("p2_rows"), 16)

            def nothing(c, full):
                pass

            def turn2(c, full):
                pe.wait_ge(sem("p2_sum"), c + 1)
                wait_past(pe, "p2_shifted", c)
                for t in range(width(full) // P):
                    last = nc.tensor.transpose(bank(3, 4 * D, P)[:, t * D:(t + 1) * D], aggT[:, t * P:(t + 1) * P], identf[:])
                last.then_inc(sem("p2_turned"), 1)
            staged(2, None, [(bank(2), hbz, D, 0)], [nothing, turn2])

            pe.wait_ge(sem("p2_low"), NCH)
            pe.wait_ge(sem("w0_in"), 16)
            if slow:
                pe.wait_ge(sem("p3_rows"), 16)

            def own3(c, full):
                wait_past(pe, "p3_ownT", c)
                own(ha, D, 0, 3, c, full).then_inc(sem("p3_own"), 1)

            def hidden3(c, full):
                n = width(full)
                pe.wait_ge(sem("p3_ownT"), c + 1)
                pe.wait_ge(sem("p3_agg_out"), c + 1)
                wait_past(pe, "p3_relu", 2 * c)
                for m in range(2):
                    dense(4 + m, n, [(wts[:, 256 + m * 128:384 + m * 128], aggT[:, C:C + n]),
                                     (wts[:, m * 128:m * 128 + 128], aggT[:, 0:n])]).then_inc(sem("p3_h3"), 1)

            def turn3(c, full):
                pe.wait_ge(sem("p3_relu"), 2 * c + 2)
                wait_past(pe, "p3_low", 2 * c)
                for k, (t0, t1) in enumerate(HALVES[full]):
                    for t in range(t0, t1):
                        for m in range(2):
                            at = ((t - t0) * 2 + m) * 128
                            last = nc.tensor.transpose(bank(6 + k, 4 * D, P)[:, at:at + 128],
                                                       actT[:, m * C + t * P:m * C + (t + 1) * P], identf[:])
                    last.then_inc(sem("p3_turned"), 1)
            staged(3, None, [(bank(2), ha, D, 0)], [own3, hidden3, turn3])

            l1v = w4[:, 0:512].rearrange("p (k o) -> p k o", k=2)
            r1v = w4[:, 512:1024].rearrange("p (k o) -> p k o", k=2)
            av = w4[:, 1024:1536].rearrange("p (k o) -> p k o", k=2)
            bv = w4[:, 1536:1792].rearrange("p (k o) -> p k o", k=2)
            h3T = wts[:, 0:2 * C]
            pe.wait_ge(sem("p3_low"), 2 * NCH - 1)
            if slow:
                pe.wait_ge(sem("p4_rows"), 16)

            def own4(c, full):
                wait_past(pe, "p4_lin2T", c)
                own(hbz, H, 0, 2, c, full).then_inc(sem("p4_own"), 1)
                wait_past(pe, "p4_sum", c)
                own(hbz, H, 1, 3, c, full).then_inc(sem("p4_own"), 1)

            def hidden4(c, full):
                n = width(full)
                pe.wait_ge(sem("w4_in"), 16)
                pe.wait_ge(sem("p4_ownT"), 2 * c + 2)
                pe.wait_ge(sem("p4_agg_out"), 2 * c + 2)
                wait_past(pe, "p4_relu", 2 * c)
                for m in range(2):
                    o = slice(m * 128, m * 128 + 128)
                    dense(4 + m, n, [(r1v[:, 0, o], h3T[:, 0:n]), (r1v[:, 1, o], h3T[:, C:C + n]),
                                     (l1v[:, 0, o], aggT[:, 0:n]), (l1v[:, 1, o], aggT[:, C:C + n])]).then_inc(sem("p4_h4"), 1)

            def lin1(c, full):
                n = width(full)
                pe.wait_ge(sem("p4_relu"), 2 * c + 2)
                wait_past(pe, "p4_relu2", 2 * c)
                for m in range(2):
                    o = slice(m * 128, m * 128 + 128)
                    dense(6 + m, n, [(av[:, k, o], actT[:, k * C:k * C + n]) for k in range(2)]).then_inc(sem("p4_lin1"), 1)

            def lin2(c, full):
                n = width(full)
                pe.wait_ge(sem("p4_relu2"), 2 * c + 2)
                dense(2, n, [(bv[:, k, :], aggT[:, k * C:k * C + n]) for k in range(2)]).then_inc(sem("p4_lin2"), 1)

            def turn4(c, full):
                pe.wait_ge(sem("p4_lin2T"), c + 1)
                for t in range(width(full) // P):
                    last = nc.tensor.transpose(bank(3, 4 * D, P)[:, t * D:(t + 1) * D], h3T[:, t * P:(t + 1) * P], identf[:])
                last.then_inc(sem("p4_turned"), 1)
            staged(4, None, [(bank(0), hbz, H, 0), (bank(1), hbz, H, 1)], [own4, hidden4, lin1, lin2, turn4])

        @block.sync
        def _(sp):
            sp.dma_start(dst_i, dst.rearrange("(r e) -> r e", r=ER)).then_inc(sem("dst_in"), 16)
            sp.dma_start(src_i, src.rearrange("(r e) -> r e", r=ER)).then_inc(sem("src_in"), 16)
            sp.dma_start(tiles(xs0, D), x.rearrange("(t p) d -> p t d", p=P)).then_inc(sem("x_in"), 16)
            n = 0
            for name, w in (("l0", Wl0), ("r0", Wr0), ("l1", Wl1), ("r1", Wr1), ("a", Wa), ("b", Wb)):
                at, kt, mt = WN[name]
                sp.dma_start(wn[:, at:at + kt * mt * 128].rearrange("p (m k) -> p m k", m=mt),
                             w.rearrange("(m p) k -> p m k", p=128)).then_inc(sem("w_in"), 16)
                n += 1
            sp.dma_start(w1v, W1.rearrange("(k p) o -> p k o", p=128)).then_inc(sem("w_in"), 16)
            sp.dma_start(w2v, W2.rearrange("(k p) o -> p k o", p=128)).then_inc(sem("w_in"), 16)
            for dstc, b, k in ((b1c, b1, 2), (bl0c, bl0, 2), (bl1c, bl1, 2), (bac, ba, 2), (b2c, b2, 1), (bbc, bb, 1)):
                with nc.allow_non_contiguous_dma(reason="one bias per partition"):
                    sp.dma_start(dstc, b.rearrange("(k p) -> p k", k=k)).then_inc(sem("w_in"), 16)
            sp.wait_ge(sem("keys"), 1)
            sp.dma_start(key_d[0:E].rearrange("(r e) -> r e", r=ER), keyf).then_inc(sem("key_out"), 16)
            sp.wait_ge(sem("padk"), 1)
            sp.dma_start(key_d[E:E + 250].rearrange("(o e) -> o e", o=1), padk[0:1, 0:250]).then_inc(sem("key_out"), 16)
            sp.wait_ge(sem("wt"), 5)
            sp.dma_start(wt_d, wt_s).then_inc(sem("wt_out"), 16)
            branch(sp, sp_layers)

        @block.gpsimd
        def _(pool):
            nc.gpsimd.memset(identf[:], 0.0).then_inc(sem("pool"), 1)
            nc.gpsimd.memset(identh[:], 0.0).then_inc(sem("pool"), 1)
            nc.gpsimd.memset(padk[:, :], 1.2e7).then_inc(sem("padk"), 1)
            nc.gpsimd.memset(onesf[:, :], 1.0).then_inc(sem("ones"), 1)
            nc.gpsimd.memset(ones_c, 1.0).then_inc(sem("ones"), 1)
            nc.gpsimd.memset(epsc, 1e-5).then_inc(sem("ones"), 1)
            pool.wait_ge(sem("pool"), 2)
            for t in (identf, identh):
                nc.gpsimd.affine_select(out=t[:], in_=t[:], compare_op=ALU.not_equal, fill=1.0, base=0,
                                        pattern=[[-1, 128]], channel_multiplier=1).then_inc(sem("ident"), 1)
            nc.gpsimd.iota(thr, [[WD * P, QG]], base=0, channel_multiplier=WD,
                           allow_small_or_imprecise_dtypes=True).then_inc(sem("iota"), 1)
            nc.gpsimd.iota(iota_h, [[1, 128]], base=0, channel_multiplier=0,
                           allow_small_or_imprecise_dtypes=True).then_inc(sem("iota"), 1)
            pool.wait_ge(sem("rowi"), 1)
            pool.wait_ge(sem("key_out"), 32)
            for g in range(QG):
                pool.indirect_dma_start(rows[:, g * EC:(g + 1) * EC], None,
                                        key_d[0:E].rearrange("(r e) -> r e", e=EC),
                                        bass.IndirectOffsetOnAxis(rowi[:, g:g + 1], 0)).then_inc(sem(f"rows{g}"), 16)
            pool.wait_ge(sem("starti"), 1)
            for g in range(QG):
                pool.indirect_dma_start(gk[:, g * CAP:(g + 1) * CAP], None,
                                        key_d.rearrange("(e o) -> e o", o=1),
                                        bass.IndirectOffsetOnAxis(starti[:, g:g + 1], 0)).then_inc(sem(f"gk{g}"), 16)
            branch(pool, pool_layers)

        @block.vector
        def _(dve):
            lk = Link(dve, "dve")
            dve.wait_ge(sem("dst_in"), 16)
            nc.vector.tensor_copy(dstf, dst_i).then_inc(sem("dstf"), 1)
            dve.wait_ge(sem("src_in"), 16)
            lk(nc.vector.tensor_scalar(t_i, src_i, float(DIV_M), None, ALU.mult))
            lk(nc.vector.tensor_scalar(s_i, t_i, DIV_S, None, ALU.logical_shift_right))
            dve.wait_ge(sem("dstf"), 1)
            lk(nc.vector.scalar_tensor_tensor(keyf, dstf, float(S * KEY), src_i, ALU.mult, ALU.add))
            nc.vector.scalar_tensor_tensor(keyf, s_i, float(KEY - P), keyf, ALU.mult, ALU.add).then_inc(sem("keys"), 1)
            dve.wait_ge(sem("ident"), 2)
            nc.vector.tensor_scalar(diag, identf[0:ER, 0:ER], dstf[:, 0:1], None, ALU.mult).then_inc(sem("diag"), 1)
            dve.wait_ge(sem("iota"), 2)
            dve.wait_ge(sem("firsts"), 1)
            for g in range(QG):
                last = nc.vector.tensor_scalar(scr[0:P, 0:ER], bank(0, ER, P), thr[:, g:g + 1], None, ALU.is_lt, ALU.add,
                                               accum_out=rowf[:, g:g + 1])
                lk(last)
            lk(nc.vector.tensor_scalar(rowf, rowf, -1.0, 0.0, ALU.add, ALU.max))
            nc.vector.tensor_copy(rowi, rowf).then_inc(sem("rowi"), 1)
            lk(nc.vector.tensor_scalar(wbase, thr, float(S * KEY), None, ALU.mult))
            dve.wait_ge(sem("x_in"), 16)

            def starts():
                for g in range(QG):
                    dve.wait_ge(sem(f"rows{g}"), 16)
                    lk(nc.vector.tensor_scalar(scr[0:P, 0:EC], rows[:, g * EC:(g + 1) * EC], wbase[:, g:g + 1], None,
                                               ALU.is_lt, ALU.add, accum_out=cnt[:, g:g + 1]))
                lk(nc.vector.scalar_tensor_tensor(rowf, rowf, float(EC), cnt[:, 0:QG], ALU.mult, ALU.add))
                nc.vector.tensor_copy(starti, rowf).then_inc(sem("starti"), 1)
            ln_dve(dve, lk, "n_", 1, xs0, xc0, sq0, st0, S, h0v[:, :, 0, :], h0v[:, :, 1, :], before=starts)
            for g in range(QG):
                dve.wait_ge(sem(f"gk{g}"), 16)
                v = gk[:, g * CAP:(g + 1) * CAP]
                nc.vector.tensor_scalar(v, v, wbase[:, g:g + 1], None, ALU.subtract).then_inc(sem("relative"), 1)
            dve.wait_ge(sem("relative"), QG)
            c3 = cnt[:, 0:(WD + 1) * QG].rearrange("p (g j) -> p g j", j=WD + 1)
            for g in range(QG):
                for j in range(WD + 1):
                    last = nc.vector.tensor_scalar(scr[0:P, 0:CAP], gk[:, g * CAP:(g + 1) * CAP], float(j * S * KEY), None,
                                                   ALU.is_lt, ALU.add, accum_out=c3[:, g, j:j + 1])
                    lk(last)
            d3 = deg.rearrange("p (g j) -> p g j", j=WD)
            lk(nc.vector.tensor_tensor(d3, c3[:, :, 1:WD + 1], c3[:, :, 0:WD], ALU.subtract))
            nc.vector.tensor_reduce(flag_f[0:P], deg, AX, ALU.add).then_inc(sem("held"), 1)
            lk(nc.vector.tensor_scalar(deg, deg, 1.0, None, ALU.max))
            nc.vector.reciprocal(deg, deg).then_inc(sem("inverse"), 1)
            dve.wait_ge(sem("held_sum"), 1)
            nc.vector.tensor_scalar(flag_i[0:1], bank(1, 1, 1), float(E), None, ALU.is_equal).then_inc(sem("flag"), 1)
            dve.wait_ge(sem("keysT"), 1)
            lk(nc.vector.tensor_copy(k_i[:, 0:4 * P], bank(2, 4 * P)))
            lk(nc.vector.tensor_copy(k_i[:, 4 * P:NWIN], bank(3, P)))
            lk(nc.vector.tensor_scalar(kp_i, k_i, KEY - 1, None, ALU.bitwise_and))
            lk(nc.vector.tensor_copy(kp[:, :], kp_i))
            lk(nc.vector.tensor_scalar(k_i, k_i, 7, None, ALU.arith_shift_right))
            lk(nc.vector.tensor_copy(kn[:, :], k_i))
            dve.wait_ge(sem("w_in"), 16 * NW)
            wa = scr[:, 0:512]
            lk(nc.vector.tensor_reduce(bnd, wn[:, 0:256].rearrange("p (m k) -> p m k", m=2), AX, ALU.add, apply_absolute_value=True))
            lk(nc.vector.tensor_reduce(tmp2, wn[:, 256:512].rearrange("p (m k) -> p m k", m=2), AX, ALU.add, apply_absolute_value=True))
            lk(nc.vector.tensor_tensor(bnd, bnd, tmp2, ALU.add))
            lk(absolute(tmp2, bl0c))
            lk(nc.vector.scalar_tensor_tensor(bnd, bnd, LN_BOUND, tmp2, ALU.mult, ALU.add))

            def pow2(scale, inverse, bound):
                lk(nc.vector.tensor_scalar(bound, bound, 1e-20, None, ALU.max))
                lk(nc.vector.reciprocal(bound, bound))
                lk(nc.vector.tensor_scalar(bound, bound, TOP, None, ALU.mult))
                lk(nc.vector.tensor_scalar(scale.bitcast(I32), bound.bitcast(I32), EXP_MASK, None, ALU.bitwise_and))
                lk(nc.vector.tensor_scalar(inverse.bitcast(I32), scale.bitcast(I32), -1.0, float(EXP_FLIP), ALU.mult, ALU.add))
            pow2(s3, is3, bnd)
            lk(nc.vector.tensor_tensor(b3s, bl0c, s3, ALU.mult))
            nc.vector.tensor_copy(tmp3, is3).then_inc(sem("scale3"), 1)
            lk(absolute(wa, wts[:, 0:512]))
            absolute(scr[:, 512:768], wts[:, 768:1024]).then_inc(sem("absw"), 1)
            lk(absolute(tmp2, b1c))
            dve.wait_ge(sem("bound1"), 1)
            nc.vector.scalar_tensor_tensor(bnd, bank(0, 2), LN_BOUND, tmp2, ALU.mult, ALU.add).then_inc(sem("bound1s"), 1)
            dve.wait_ge(sem("boundz"), 1)
            lk(nc.vector.tensor_copy(bndz, bank(0, 3)[:, 2:3]))
            pow2(zs, izs, bndz)
            nc.vector.tensor_scalar(wts[:, 0:512], wts[:, 0:512], 1.0 / LN_SCALE, None, ALU.mult).then_inc(sem("w1_scaled"), 1)
            branch(dve, dve_layers)

        @block.scalar
        def _(act):
            act.wait_ge(sem("ones"), 3)
            ln_act(act, "n_", 1, xc0, sq0, st0, S, h0v[:, :, 0, :])
            act.wait_ge(sem("scale3"), 1)
            for k in range(5):
                act.wait_ge(sem("wturned"), k + 1)
                if k == 0:
                    nc.scalar.activation(wt_s[:, 0:512], bank(4), ACT.Copy, scale=1.0 / LN_SCALE).then_inc(sem("wt"), 1)
                elif k < 3:
                    for kt in range(2):
                        last = nc.scalar.activation(wt_s[:, 512 * k + 256 * kt:512 * k + 256 * kt + 256],
                                                    bank(4 + k % 2)[:, 256 * kt:256 * kt + 256], ACT.Identity, scale=is3[:, kt:kt + 1])
                    last.then_inc(sem("wt"), 1)
                else:
                    n = 512 if k == 3 else 256
                    nc.scalar.activation(wt_s[:, 512 * k:512 * k + n], bank(4 + k % 2, n), ACT.Copy).then_inc(sem("wt"), 1)
            branch(act, act_layers)

        @block.tensor
        def _(pe):
            pe.wait_ge(sem("ones"), 3)
            pe.wait_ge(sem("ident"), 2)
            pe.wait_ge(sem("diag"), 1)
            nc.tensor.matmul(bank(0, ER, P), onesf[0:ER, 0:P], diag, start=True, stop=True).then_inc(sem("firsts"), 1)
            pe.wait_ge(sem("relative"), QG)
            for g in range(QG):
                at = 2 * BANK + g * P if g < 4 else 3 * BANK
                last = nc.tensor.transpose(ps[:, at:at + P], gk[:, g * CAP:(g + 1) * CAP], identf[0:P, 0:P])
            last.then_inc(sem("keysT"), 1)
            pe.wait_ge(sem("held"), 1)
            nc.tensor.matmul(bank(1, 1, 1), flag_f[0:P], onesf[0:P, 0:1], start=True, stop=True).then_inc(sem("held_sum"), 1)
            pe.wait_ge(sem("w_in"), 16 * NW)
            blocks = []
            for name in ("l0", "r0", "l1", "r1", "a", "b"):
                at, kt, mt = WN[name]
                for k in range(kt):
                    for m in range(mt):
                        blocks.append(wn[:, at + (m * kt + k) * 128:at + (m * kt + k) * 128 + 128])
            for n, b in enumerate(blocks):
                if n % 4 == 0 and n >= 8:
                    pe.wait_ge(sem("wt"), n // 4 - 1)
                last = nc.tensor.transpose(bank(4 + (n // 4) % 2)[:, (n % 4) * 128:(n % 4) * 128 + 128], b, identf[:])
                if n % 4 == 3 or n == len(blocks) - 1:
                    last.then_inc(sem("wturned"), 1)
            pe.wait_ge(sem("absw"), 1)
            for m in range(2):
                for k in range(2):
                    last = nc.tensor.matmul(bank(0)[:, m:m + 1], scr[:, k * 256 + m * 128:k * 256 + m * 128 + 128], ones_c,
                                            start=(k == 0), stop=(k == 1))
            last.then_inc(sem("bound1"), 1)
            pe.wait_ge(sem("bound1s"), 1)
            for m in range(2):
                last = nc.tensor.matmul(bank(0)[:, 2:3], scr[:, 512 + m * 128:640 + m * 128], bnd[:, m:m + 1],
                                        start=(m == 0), stop=(m == 1))
            last.then_inc(sem("boundz"), 1)
            branch(pe, pe_layers)


_INS = ["x", "src", "dst", "L0_gnn_W1", "L0_gnn_b1", "L0_gnn_W2", "L0_gnn_b2", "L1_gnn_W_l0", "L1_gnn_b_l0", "L1_gnn_W_r0",
        "L1_gnn_W_l1", "L1_gnn_b_l1", "L1_gnn_W_r1", "L1_gnn_W_lin1", "L1_gnn_b_lin1", "L1_gnn_W_lin2", "L1_gnn_b_lin2"]


def kernel(**inputs):
    import numpy as _np
    import concourse.bacc as _bacc
    from concourse import mybir as _mybir
    from concourse.bass_utils import run_bass_kernel_spmd as _run

    nc = _bacc.Bacc("TRN2", target_bir_lowering=False, num_devices=1)
    arrays, args = {}, []
    for name in _INS:
        a = _np.ascontiguousarray(inputs[name])
        arrays[f"in_{name}_dram"] = a
        args.append(nc.dram_tensor(f"in_{name}_dram", a.shape, _mybir.dt.from_np(a.dtype), kind="ExternalInput").ap())
    out = nc.dram_tensor("out_0_dram", (N, D), _mybir.dt.float32, kind="ExternalOutput").ap()
    sage_program(nc, *args, out)
    r = _run(nc, [arrays], core_ids=[0])
    return r.results[0]["out_0_dram"]
```

```python
from contextlib import ExitStack

import concourse.bass as bass
from concourse import mybir

F32 = mybir.dt.float32
F16 = mybir.dt.float16
I32 = mybir.dt.int32
ALU = mybir.AluOpType
ACT = mybir.ActivationFunctionType
AX = mybir.AxisListType.X
ds = bass.ds

N = 3125
E = 50000
D = 128
H = 256
P = 125
S = N // P
ER = 125
EC = E // ER

WD = 5
NWIN = N // WD
KEY = 128
WKEY = WD * S * KEY
CAP = 128
GW = 4
QG = NWIN // P
DIV_M, DIV_S = 4195, 19

C = 500
NFULL = N // C
NCH = NFULL + 1
BANK = 512
NW = 14
HALVES = {True: ((0, 2), (2, 4)), False: ((0, 1),)}
LN_SCALE = 4096.0
LN_BOUND = 11.5
TOP = 32768.0
CUT1, CUT2 = 8, 16
EXP_MASK = 0x7F800000
EXP_FLIP = 254 << 23


def width(full):
    return C if full else N - NFULL * C


def sage_program(nc, x, src, dst, W1, b1, W2, b2, Wl0, bl0, Wr0, Wl1, bl1, Wr1, Wa, ba, Wb, bb, out):
    ctx = ExitStack()
    with ctx:
        def sb(name, cols, dt=F32):
            return ctx.enter_context(nc.sbuf_tensor(name, [128, cols], dt))

        sems = {}

        def sem(name):
            if name not in sems:
                sems[name] = ctx.enter_context(nc.semaphore(name))
            return sems[name]

        def over(t, at, cols, dt):
            n = cols * (2 if dt == F16 else 4) // 2
            v = t[:, at // 2:at // 2 + n]
            return v if dt == F16 else v.bitcast(dt)

        key_d = nc.dram_tensor("key_d", [E + ER * 2], F32, kind="Internal").ap()
        inv_d = nc.dram_tensor("inv_d", [N], F32, kind="Internal").ap()
        wt_d = nc.dram_tensor("wt_d", [128, 2304], F32, kind="Internal").ap()
        self_d = nc.dram_tensor("self_d", [128, N], F32, kind="Internal").ap()
        x1_d = nc.dram_tensor("x1_d", [N, D], F32, kind="Internal").ap()
        hs_d1 = nc.dram_tensor("hs_d1", [N, 2 * D], F16, kind="Internal").ap()
        hs_d2 = nc.dram_tensor("hs_d2", [N, 2 * D], F16, kind="Internal").ap()
        hs_d3 = nc.dram_tensor("hs_d3", [N, 2 * D], F16, kind="Internal").ap()
        hs_d4 = nc.dram_tensor("hs_d4", [N, 2 * H], F16, kind="Internal").ap()

        adj = sb("adj", S * N + 1, F16)
        hs_a = sb("hs_a", S * 2 * D, F16)
        hs_b = sb("hs_b", S * 2 * H, F16)
        wts = sb("wts", 1024)
        invc = sb("invc", C)
        aggT = sb("aggT", 2 * C)
        actT = sb("actT", 2 * C)
        zT = sb("zT", C)
        identf = sb("identf", 128)
        identh = sb("identh", 128, F16)
        st = sb("st", 64)
        col = sb("col", 40)
        ps = ctx.enter_context(nc.psum_tensor("ps", [128, 8 * BANK], F32))

        def bank(i, cols=BANK, rows=128):
            return ps[0:rows, i * BANK:i * BANK + cols]

        b1c, b2c, bl0c, bl1c, bac, bbc = (col[:, 0:2], col[:, 2:3], col[:, 3:5], col[:, 5:7], col[:, 7:9], col[:, 9:10])
        s3, is3, b3s = col[:, 10:12], col[:, 12:14], col[:, 14:16]
        zs, izs = col[:, 16:17], col[:, 17:18]
        bnd = col[:, 18:20]
        tmp2 = col[:, 20:22]
        epsc = col[:, 22:23]
        ones_c = col[:, 23:24]
        flag_f = col[:, 24:25]
        flag_i = col[:, 25:26].bitcast(I32)
        bndz = col[:, 26:27]
        tmp3 = col[:, 28:30]

        o = [0]

        def lay(cols, dt):
            at = o[0]
            o[0] += (cols * (2 if dt == F16 else 4) + 63) // 64 * 64
            return over(adj, at, cols, dt)
        dst_i, src_i, t_i, s_i = (lay(EC, I32)[0:ER] for _ in range(4))
        dstf, keyf, dstrel = (lay(EC, F32)[0:ER] for _ in range(3))
        rows = lay(QG * EC, F32)[0:P]
        gk = lay(QG * CAP, F32)[0:P]
        scr = lay(2 * H * QG, F32)
        xs0, xc0, sq0 = (lay(S * D, F32)[0:P] for _ in range(3))
        wn = lay(2304, F32)
        wt_s = lay(2304, F32)
        thr = lay(QG, F32)[0:P]
        wbase = lay(QG, F32)[0:P]
        cnt = lay(8 * QG, F32)[0:P]
        rowi = lay(QG, I32)[0:P]
        rowf = lay(QG, F32)[0:P]
        starti = lay(QG, I32)[0:P]
        diag = lay(ER, F32)[0:ER]
        onesf = lay(128, F32)
        deg = lay(QG * WD, F32)[0:P]
        st0 = lay(S * 4, F32)[0:P]
        k_i = lay(NWIN, I32)
        kp_i = lay(NWIN, I32)
        padk = lay(256, F32)
        iota5 = lay(C, F16)[0:ER]
        zeros = lay(C, F16)[0:ER]
        onesh = lay(128, F16)[0:ER]
        oh = lay(C, F16)[0:ER]
        gbuf = lay(2 * H, F16)[0:ER]
        idx = lay(1, I32)[0:ER]
        assert o[0] <= S * N * 2
        up = S * 2 * D * 2
        kp = over(hs_b, up, NWIN, F16)
        kn = over(hs_b, up + 1280, NWIN, F16)
        onehot = lambda at: over(hs_b, up + at, 128 * GW, F16).rearrange("p (v w) -> p v w", w=GW)
        ohp = [onehot(2560 + 1024 * i) for i in range(2)]
        ohn = [onehot(4608 + 1024 * i) for i in range(2)]
        iota4 = onehot(6656)
        selfT = over(hs_b, up + 7680, C, F32)
        xin, yc, sqb, x1b, hb = (over(hs_b, up + 2048 * i, 4 * D, F32)[0:P] for i in range(5))
        selfc = over(hs_b, up + 10240, C, F32)
        w4 = over(hs_a, 0, 1792, F32)
        x1in = over(hs_a, 7168, 4 * D, F32)[0:P]
        outb = over(hs_a, 9216, 4 * D, F32)[0:P]

        w1v = wts[:, 0:512].rearrange("p (k o) -> p k o", k=2)
        w2v = wts[:, 512:1024].rearrange("p (k o) -> p k o", k=4)
        ha = hs_a[0:P]
        hbz = hs_b[0:P]

        def tiles(t, w):
            return t.rearrange("p (t d) -> p t d", d=w)

        def absolute(o, v):
            return nc.vector.tensor_scalar(o.bitcast(I32), v.bitcast(I32), 0x7FFFFFFF, None, ALU.bitwise_and)

        def hs_write(h, c, full, part, w):
            n = width(full) // P
            v = h[:, ds(c * (4 * 2 * w), n * 2 * w)].rearrange("p (t k d) -> p t k d", k=2, d=w)
            return v[:, :, part, :]

        class Link:

            def __init__(self, eng, name, base=0):
                self.eng, self.sem, self.base, self.n = eng, sem(name), base, 0

            def __call__(self, ins):
                self.n += 1
                ins.then_inc(self.sem, 1)
                self.eng.wait_ge(self.sem, self.base + self.n)

        def wait_past(eng, name, value):
            if not isinstance(value, int) or value > 0:
                eng.wait_ge(sem(name), value)

        def chunks(eng, emit):
            emit(0, True)
            with eng.Fori(1, NFULL) as c:
                emit(c, True)
            emit(NFULL, False)

        def ln_dve(dve, lk, p, k, X, XC, SQ, stat, T, hi, lo, before=None):
            m, v = stat[:, 0:T], stat[:, T:2 * T]
            bc = lambda a: a.unsqueeze(2).to_broadcast([P, T, D])
            X3, XC3, SQ3 = (tiles(t, D) for t in (X, XC, SQ))
            lk(nc.vector.tensor_reduce(m, X3, AX, ALU.add))
            lk(nc.vector.tensor_scalar(m, m, 1.0 / D, None, ALU.mult))
            nc.vector.tensor_tensor(XC3, X3, bc(m), ALU.subtract).then_inc(sem(p + "centred"), 1)
            if before:
                before()
            dve.wait_ge(sem(p + "squares"), k)
            nc.vector.tensor_reduce(v, SQ3, AX, ALU.add).then_inc(sem(p + "sumsq"), 1)
            dve.wait_ge(sem(p + "std"), k)
            lk(nc.vector.reciprocal(v, v))
            lk(nc.vector.tensor_scalar(v, v, LN_SCALE, None, ALU.mult))
            dve.wait_ge(sem(p + "centred"), k)
            nc.vector.tensor_tensor(SQ3, XC3, bc(v), ALU.mult).then_inc(sem(p + "normed"), 1)
            dve.wait_ge(sem(p + "high"), k)
            nc.vector.scalar_tensor_tensor(lo, SQ3, 0.0, hi, ALU.max, ALU.subtract).then_inc(sem(p + "low"), 1)

        def ln_act(act, p, k, XC, SQ, stat, T, hi):
            v = stat[:, T:2 * T]
            act.wait_ge(sem(p + "centred"), k)
            nc.scalar.activation(SQ, XC, ACT.Square).then_inc(sem(p + "squares"), 1)
            act.wait_ge(sem(p + "sumsq"), k)
            nc.scalar.activation(v, v, ACT.Sqrt, bias=epsc[0:P], scale=1.0 / D).then_inc(sem(p + "std"), 1)
            act.wait_ge(sem(p + "normed"), k)
            nc.scalar.activation(hi, tiles(SQ, D), ACT.Relu).then_inc(sem(p + "high"), 1)

        block = ctx.enter_context(nc.Block())

        h0v = ha.rearrange("p (t k d) -> p t k d", k=2, d=D)
        WN = {"l0": (0, 1, 2), "r0": (256, 1, 2), "l1": (512, 2, 2), "r1": (1024, 2, 2), "a": (1536, 2, 2), "b": (2048, 2, 1)}

        def sp_layers(sp, slow):
            if not slow:
                sp.wait_ge(sem("inverse"), 1)
                with nc.allow_non_contiguous_dma(reason="runs of 5 inverse degrees"):
                    sp.dma_start(inv_d.rearrange("(g q j) -> q g j", q=P, j=WD),
                                 deg.rearrange("q (g j) -> q g j", j=WD)).then_inc(sem("inv_out"), 16)
            else:
                def store_inv(c, full):
                    sp.wait_ge(sem("sd_inv"), c + 1)
                    sp.dma_start(inv_d[ds(c * C, width(full))].rearrange("(o e) -> o e", o=1),
                                 invc[0:1, 0:width(full)]).then_inc(sem("inv_out"), 16)
                    sp.wait_ge(sem("inv_out"), 16 * c + 16)
                    sp.sem_inc(sem("inv_out_seen"), 1)
                chunks(sp, store_inv)
            ninv = NCH if slow else 1
            sp.wait_ge(sem("inv_out"), 16 * ninv)

            def load_inv(p, c, full):
                sp.dma_start(invc[:, 0:width(full)],
                             inv_d[ds(c * C, width(full))].partition_broadcast(128)).then_inc(sem(p + "inv"), 16)

            def spread(ph, hs, w, hd):
                if slow:
                    sp.dma_start(hd.rearrange("(t p) f -> p t f", p=P),
                                 hs.rearrange("p (t f) -> p t f", f=2 * w)).then_inc(sem(f"p{ph}_rows"), 16)

            def each(emit):
                emit(0, True, True)
                with sp.Fori(1, NFULL - 1) as c:
                    emit(c, True, True)
                emit(NFULL - 1, True, False)
                emit(NFULL, False, None)

            sp.wait_ge(sem("n_low"), 1)
            spread(1, ha, D, hs_d1)
            load_inv("p1_", 0, True)

            def step1(c, full, nxt):
                sp.wait_ge(sem("p1_agg_out"), c + 1)
                if nxt is not None:
                    load_inv("p1_", c + 1, nxt)
                sp.wait_ge(sem("p1_self"), c + 1)
                sp.dma_start(self_d[:, ds(c * C, width(full))], selfT[:, 0:width(full)]).then_inc(sem("p1_self_out"), 16)
            each(step1)
            sp.wait_ge(sem("p1_h1"), 2 * NCH)
            sp.wait_ge(sem("wt_out"), 16)
            sp.dma_start(wts[:, 0:512], wt_d[:, 0:512]).then_inc(sem("w0_in"), 16)
            sp.wait_ge(sem("p1_self_out"), 16 * NCH)
            sp.wait_ge(sem("p1_low"), NCH)
            spread(2, hbz[:, 0:S * 2 * D], D, hs_d2)

            def load_self(c, full):
                sp.dma_start(selfc[:, 0:width(full)], self_d[:, ds(c * C, width(full))]).then_inc(sem("p2_self"), 16)

            def load_x(c, full):
                sp.dma_start(tiles(xin[:, 0:width(full) // P * D], D),
                             x[ds(c * C, width(full)), :].rearrange("(t p) d -> p t d", p=P)).then_inc(sem("p2_x"), 16)
            load_inv("p2_", 0, True)
            load_self(0, True)
            load_x(0, True)

            def step2(c, full, nxt):
                if nxt is not None:
                    sp.wait_ge(sem("p2_agg_out"), c + 1)
                    load_inv("p2_", c + 1, nxt)
                    sp.wait_ge(sem("p2_sum"), c + 1)
                    load_self(c + 1, nxt)
                    sp.wait_ge(sem("p2_x_used"), c + 1)
                    load_x(c + 1, nxt)
                sp.wait_ge(sem("p2_x1"), c + 1)
                sp.dma_start(x1_d[ds(c * C, width(full)), :].rearrange("(t p) d -> p t d", p=P),
                             tiles(x1b[:, 0:width(full) // P * D], D)).then_inc(sem("p2_x1_out"), 16)
            each(step2)
            sp.wait_ge(sem("p2_x1_out"), 16 * NCH)
            sp.wait_ge(sem("p2_low"), NCH)
            spread(3, ha, D, hs_d3)
            load_inv("p3_", 0, True)

            def step3(c, full, nxt):
                if nxt is not None:
                    sp.wait_ge(sem("p3_agg_out"), c + 1)
                    load_inv("p3_", c + 1, nxt)
            each(step3)
            sp.wait_ge(sem("p3_agg_out"), NCH)
            sp.wait_ge(sem("p3_own"), NCH)
            if slow:
                sp.wait_ge(sem("p3_rows"), 16)
            sp.dma_start(w4, wt_d[:, 512:2304]).then_inc(sem("w4_in"), 16)
            sp.wait_ge(sem("p3_low"), 2 * NCH - 1)
            spread(4, hbz, H, hs_d4)
            load_inv("p4_", 0, True)

            def load_x1(c, full):
                sp.dma_start(tiles(x1in[:, 0:width(full) // P * D], D),
                             x1_d[ds(c * C, width(full)), :].rearrange("(t p) d -> p t d", p=P)).then_inc(sem("p4_x1"), 16)
            load_x1(0, True)

            def step4(c, full, nxt):
                sp.wait_ge(sem("p4_agg_out"), 2 * c + 2)
                if nxt is not None:
                    load_inv("p4_", c + 1, nxt)
                sp.wait_ge(sem("p4_sum"), c + 1)
                sp.dma_start(out[ds(c * C, width(full)), :].rearrange("(t p) d -> p t d", p=P),
                             tiles(outb[:, 0:width(full) // P * D], D)).then_inc(sem("p4_out"), 16)
                if nxt is not None:
                    load_x1(c + 1, nxt)
            each(step4)
            sp.wait_ge(sem("p4_out"), 16 * NCH)

        def branch(eng, layers):
            eng.wait_ge(sem("flag"), 1)
            fits = eng.value_load(flag_i[0:1, 0:1], min_val=0, max_val=1)
            with eng.If(fits == 1):
                layers(eng, False)
            with eng.Else():
                layers(eng, True)

        def pool_layers(pool, slow):
            if not slow:
                return
            nc.gpsimd.iota(iota5, [[1, C]], base=0, channel_multiplier=0,
                           allow_small_or_imprecise_dtypes=True).then_inc(sem("slow_consts"), 1)
            nc.gpsimd.memset(zeros, 0.0).then_inc(sem("slow_consts"), 1)
            nc.gpsimd.memset(onesh, 1.0).then_inc(sem("slow_consts"), 1)
            for ph, hd, w in ((1, hs_d1, D), (2, hs_d2, D), (3, hs_d3, D), (4, hs_d4, H)):
                pool.wait_ge(sem(f"p{ph}_rows"), 16)
                with pool.Fori(0, NCH * EC) as u:
                    pool.wait_ge(sem(f"p{ph}_edge"), 2 * u + 2)
                    pool.sem_inc(sem(f"p{ph}_edge_seen"), 1)
                    pool.indirect_dma_start(gbuf[:, 0:2 * w], None, hd,
                                            bass.IndirectOffsetOnAxis(idx, 0)).then_inc(sem(f"p{ph}_gathered"), 16)

        def dve_slow(dve, ph, c):
            with dve.Fori(0, EC) as j:
                u = c * EC + j
                dve.wait_ge(sem(f"p{ph}_edge_used"), u + 1)
                nc.vector.tensor_copy(idx, src_i[:, ds(j, 1)]).then_inc(sem(f"p{ph}_edge"), 1)
                nc.vector.tensor_scalar(oh, iota5, dstrel[:, ds(j, 1)], None, ALU.is_equal).then_inc(sem(f"p{ph}_edge"), 1)
            dve.wait_ge(sem(f"p{ph}_edge"), 2 * EC * (c + 1))
            Link(dve, f"dve_slow{ph}", c)(nc.vector.tensor_scalar(dstrel, dstrel, float(-C), None, ALU.add))

        def pe_slow(pe, ph, c, full, accs, w):
            n = width(full)
            for a in accs:
                nc.tensor.matmul(a, zeros[:, 0:128], zeros[:, 0:n], start=True, stop=False, skip_group_check=True)
            with pe.Fori(0, EC) as j:
                u = c * EC + j
                pe.wait_ge(sem(f"p{ph}_edge"), 2 * u + 2)
                if w:
                    pe.wait_ge(sem(f"p{ph}_gathered"), 16 * u + 16)
                for h, a in enumerate(accs):
                    for part in range(2 if w else 1):
                        lhs = gbuf[:, part * w + h * 128:part * w + h * 128 + 128] if w else onesh
                        last = nc.tensor.matmul(a, lhs, oh[:, 0:n], start=False, stop=False, skip_group_check=True)
                last.then_inc(sem(f"p{ph}_edge_used"), 1)
            for a in accs:
                last = nc.tensor.matmul(a, zeros[:, 0:128], zeros[:, 0:n], start=False, stop=True, skip_group_check=True)
            return last

        def dve_layers(dve, slow):
            if slow:
                dve.wait_ge(sem("slow_consts"), 3)
                dve.sem_inc(sem("p0_edge_used"), 1)
                Link(dve, "dve_s0")(nc.vector.tensor_copy(dstrel, dstf))

                def degrees(c, full):
                    n = width(full)
                    lk = Link(dve, "dve_s1", c)
                    dve_slow(dve, 0, c)
                    dve.wait_ge(sem("p0_agg"), c + 1)
                    wait_past(dve, "inv_out", 16 * c)
                    lk(nc.vector.tensor_scalar(invc[:, 0:n], bank(2, n), 1.0, None, ALU.max))
                    nc.vector.reciprocal(invc[:, 0:n], invc[:, 0:n]).then_inc(sem("sd_inv"), 1)
                chunks(dve, degrees)

            def slow_reset(ph):
                if slow:
                    dve.sem_inc(sem(f"p{ph}_edge_used"), 1)
                    Link(dve, f"dve_s{ph + 1}")(nc.vector.tensor_copy(dstrel, dstf))

            def build(c, full):
                nw = GW if full else 1

                def group(g, k, wait):
                    wait_past(dve, "counted", wait)
                    win = g * GW if full else NFULL * S * GW + (g - NFULL * S)
                    for oh, key in ((ohp[k], kp), (ohn[k], kn)):
                        last = nc.vector.tensor_tensor(oh[:, :, 0:nw], iota4[:, :, 0:nw],
                                                       key[:, ds(win, nw)].unsqueeze(1).to_broadcast([128, 128, nw]), ALU.is_equal)
                    last.then_inc(sem("onehot"), 1)
                group(c * S, 0, c * S)
                for i in (1, 2):
                    group(c * S + i, i % 2, c * S + i - 1)
                with dve.Fori(1, (S - 1) // 2) as h:
                    group(c * S + 1 + 2 * h, 1, c * S + 2 * h)
                    group(c * S + 2 + 2 * h, 0, c * S + 1 + 2 * h)

            def agg_out(c, full):
                n = width(full)
                dve.wait_ge(sem("p1_inv"), 16 * c + 16)
                dve.wait_ge(sem("p1_agg"), c + 1)
                wait_past(dve, "p1_h1", 2 * c)
                nc.vector.tensor_tensor(aggT[:, 0:n], bank(2, n), invc[:, 0:n], ALU.mult).then_inc(sem("p1_agg_out"), 1)

            def self_out(c, full):
                n = width(full)
                dve.wait_ge(sem("p1_selfs"), c + 1)
                wait_past(dve, "p1_self_out", 16 * c)
                nc.vector.tensor_scalar(selfT[:, 0:n], bank(7, n), b2c, None, ALU.add).then_inc(sem("p1_self"), 1)

            def low(c, full):
                nt = width(full) // P
                dve.wait_ge(sem("p1_high"), c + 1)
                nc.vector.tensor_tensor(hs_write(hbz, c, full, 1, D), tiles(bank(3, nt * D, P), D),
                                        hs_write(hbz, c, full, 0, D), ALU.subtract).then_inc(sem("p1_low"), 1)

            def slow1(c, full):
                dve_slow(dve, 1, c)
                agg_out(c, full)
                self_out(c, full)
                low(c, full)

            def step1(c, full, nxt, first=False, second=False):
                if not first:
                    agg_out(c - 1, True)
                    if not second:
                        low(c - 2, True)
                if nxt is not None:
                    build(c + 1, nxt)
                if not first:
                    self_out(c - 1, True)

            slow_reset(1)
            if slow:
                chunks(dve, slow1)
            else:
                build(0, True)
                step1(0, True, True, first=True)
                step1(1, True, True, second=True)
                with dve.Fori(2, NFULL - 1) as c:
                    step1(c, True, True)
                step1(NFULL - 1, True, False)
                step1(NFULL, False, None)
                agg_out(NFULL, False)
                low(NFULL - 1, True)
                self_out(NFULL, False)
                low(NFULL, False)

            slow_reset(2)
            dve.wait_ge(sem("p1_self_out"), 16 * NCH)

            def step2(c, full):
                n = width(full)
                nt = n // P
                K2 = 5
                lk = Link(dve, "dve2", K2 * c)
                if slow:
                    dve_slow(dve, 2, c)
                o2 = aggT[:, 0:n]
                dve.wait_ge(sem("p2_inv"), 16 * c + 16)
                dve.wait_ge(sem("p2_agg"), c + 1)
                wait_past(dve, "p2_turned", c)
                nc.vector.scalar_tensor_tensor(o2, bank(2, n), izs, invc[:, 0:n], ALU.mult, ALU.mult).then_inc(sem("p2_agg_out"), 1)
                dve.wait_ge(sem("p2_agg_out"), c + 1)
                dve.wait_ge(sem("p2_self"), 16 * c + 16)
                nc.vector.tensor_tensor(o2, o2, selfc[:, 0:n], ALU.add).then_inc(sem("p2_sum"), 1)
                bc = lambda a: a.unsqueeze(2).to_broadcast([P, nt, D])
                v = lambda t: tiles(t[:, 0:nt * D], D)
                m, sm, ls = st[0:P, 8:8 + nt], st[0:P, 12:12 + nt], st[0:P, 16:16 + nt]
                y = tiles(bank(3, nt * D, P), D)
                dve.wait_ge(sem("p2_turned"), c + 1)
                lk(nc.vector.tensor_reduce(m, y, AX, ALU.max))
                nc.vector.tensor_tensor(v(yc), y, bc(m), ALU.subtract).then_inc(sem("p2_shifted"), 1)
                dve.wait_ge(sem("p2_shifted"), c + 1)
                dve.wait_ge(sem("p2_x"), 16 * c + 16)
                wait_past(dve, "p2_x1_out", 16 * c)
                nc.vector.tensor_tensor(v(x1b), v(xin), v(yc), ALU.add).then_inc(sem("p2_x_used"), 1)
                dve.wait_ge(sem("p2_exp"), c + 1)
                nc.vector.tensor_reduce(sm, v(sqb), AX, ALU.add).then_inc(sem("p2_expsum"), 1)
                dve.wait_ge(sem("p2_lse"), c + 1)
                dve.wait_ge(sem("p2_x_used"), c + 1)
                nc.vector.tensor_tensor(v(x1b), v(x1b), bc(ls), ALU.subtract).then_inc(sem("p2_x1"), 1)
                dve.wait_ge(sem("p2_x1"), c + 1)
                ln_dve(dve, lk, "p2_", c + 1, x1b[:, 0:nt * D], yc[:, 0:nt * D], sqb[:, 0:nt * D], st[0:P],
                       nt, hs_write(ha, c, full, 0, D), hs_write(ha, c, full, 1, D))
                assert lk.n == K2
            chunks(dve, step2)

            slow_reset(3)
            dve.wait_ge(sem("p2_x1_out"), 16 * NCH)

            def step3(c, full):
                n = width(full)
                nt = n // P
                if slow:
                    dve_slow(dve, 3, c)
                dve.wait_ge(sem("p3_inv"), 16 * c + 16)
                dve.wait_ge(sem("p3_agg"), c + 1)
                wait_past(dve, "p3_h3", 2 * c)
                nc.vector.tensor_tensor(aggT[:, 0:n], bank(2, n), invc[:, 0:n], ALU.mult).then_inc(sem("p3_agg_out"), 1)
                for k, (t0, t1) in enumerate(HALVES[full]):
                    dve.wait_ge(sem("p3_high"), 2 * c + k + 1)
                    nc.vector.tensor_tensor(hs_write(hbz, c, full, 1, H)[:, t0:t1], tiles(bank(6 + k, (t1 - t0) * H, P), H),
                                            hs_write(hbz, c, full, 0, H)[:, t0:t1], ALU.subtract).then_inc(sem("p3_low"), 1)
            chunks(dve, step3)

            slow_reset(4)

            def step4(c, full):
                n = width(full)
                nt = n // P
                if slow:
                    dve_slow(dve, 4, c)
                dve.wait_ge(sem("p4_inv"), 16 * c + 16)
                wait_past(dve, "p4_lin2", c)
                for h in range(2):
                    dve.wait_ge(sem("p4_agg"), 2 * c + h + 1)
                    nc.vector.tensor_tensor(aggT[:, h * C:h * C + n], bank(h, n), invc[:, 0:n], ALU.mult).then_inc(sem("p4_agg_out"), 1)
                dve.wait_ge(sem("p4_turned"), c + 1)
                dve.wait_ge(sem("p4_x1"), 16 * c + 16)
                wait_past(dve, "p4_out", 16 * c)
                nc.vector.tensor_tensor(outb[:, 0:nt * D], bank(3, nt * D, P), x1in[:, 0:nt * D], ALU.add).then_inc(sem("p4_sum"), 1)
            chunks(dve, step4)

        def act_layers(act, slow):
            def build(c, full, a, b):
                nd = C // S if full else WD

                def group(g, k):
                    act.wait_ge(sem("counted"), g + 1)
                    at = g * (C // S) if full else NFULL * C + (g - NFULL * S) * WD
                    v = adj[0:P, 0:S * N].rearrange("p (t n) -> p t n", n=N)
                    nc.scalar.activation(v[:, :, ds(at, nd)], bank(k, nd * S, P).rearrange("p (d t) -> p t d", t=S),
                                         ACT.Copy).then_inc(sem("evicted"), 1)
                if a == 0:
                    group(c * S, 0)
                with act.Fori(a // 2, b // 2) as h:
                    group(c * S + 1 + 2 * h, 1)
                    group(c * S + 2 + 2 * h, 0)

            def h0_turned(c, full):
                n = width(full)
                act.wait_ge(sem("p1_own"), c + 1)
                wait_past(act, "p1_h1", 2 * c)
                nc.scalar.activation(aggT[:, C:C + n], bank(6, n), ACT.Copy).then_inc(sem("p1_h0T"), 1)

            def relu(c, full):
                n = width(full)
                wait_past(act, "p1_selfs", c)
                for m in range(2):
                    act.wait_ge(sem("p1_h1"), 2 * c + m + 1)
                    nc.scalar.activation(actT[:, m * C:m * C + n], bank(4 + m, n), ACT.Relu, bias=b1c[:, m:m + 1]).then_inc(sem("p1_relu"), 1)

            def z_out(c, full):
                n = width(full)
                act.wait_ge(sem("p1_zm"), c + 1)
                wait_past(act, "p1_turned", c)
                nc.scalar.activation(zT[:, 0:n], bank(6, n), ACT.Identity, scale=zs).then_inc(sem("p1_zT"), 1)

            def high(c, full):
                nt = width(full) // P
                act.wait_ge(sem("p1_turned"), c + 1)
                nc.scalar.activation(hs_write(hbz, c, full, 0, D), tiles(bank(3, nt * D, P), D), ACT.Copy).then_inc(sem("p1_high"), 1)

            def whole(c, full):
                for part in (h0_turned, relu, z_out, high):
                    part(c, full)

            def step1(c, full, nxt, first=False, second=False):
                if not first:
                    h0_turned(c - 1, True)
                    if not second:
                        high(c - 2, True)
                for part, a, b in ((relu, 0, CUT1), (z_out, CUT1, CUT2), (None, CUT2, S - 1)):
                    if nxt is not None:
                        build(c + 1, nxt, a, b)
                    if part and not first:
                        part(c - 1, True)

            if slow:
                chunks(act, whole)
            else:
                act.wait_ge(sem("n_low"), 1)
                act.wait_ge(sem("wt_out"), 16)
                act.wait_ge(sem("inv_out"), 16)
                act.wait_ge(sem("onehot"), 1)
                build(0, True, 0, S - 1)
                step1(0, True, True, first=True)
                step1(1, True, True, second=True)
                with act.Fori(2, NFULL - 1) as c:
                    step1(c, True, True)
                step1(NFULL - 1, True, False)
                step1(NFULL, False, None)
                high(NFULL - 1, True)
                whole(NFULL, False)

            def step2(c, full):
                nt = width(full) // P
                v = lambda t: t[:, 0:nt * D]
                act.wait_ge(sem("p2_shifted"), c + 1)
                nc.scalar.activation(v(sqb), v(yc), ACT.Exp).then_inc(sem("p2_exp"), 1)
                act.wait_ge(sem("p2_expsum"), c + 1)
                nc.scalar.activation(st[0:P, 16:16 + nt], st[0:P, 12:12 + nt], ACT.Ln).then_inc(sem("p2_lse"), 1)
                ln_act(act, "p2_", c + 1, v(yc), v(sqb), st[0:P], nt, hs_write(ha, c, full, 0, D))
            chunks(act, step2)

            act.wait_ge(sem("p2_x1_out"), 16 * NCH)

            def step3(c, full):
                n = width(full)
                nt = n // P
                act.wait_ge(sem("p3_own"), c + 1)
                wait_past(act, "p3_h3", 2 * c)
                nc.scalar.activation(aggT[:, C:C + n], bank(3, n), ACT.Copy).then_inc(sem("p3_ownT"), 1)
                wait_past(act, "p3_turned", 2 * c)
                for m in range(2):
                    act.wait_ge(sem("p3_h3"), 2 * c + m + 1)
                    nc.scalar.activation(actT[:, m * C:m * C + n], bank(4 + m, n), ACT.Relu, bias=b3s[:, m:m + 1],
                                         scale=s3[:, m:m + 1]).then_inc(sem("p3_relu"), 1)
                for k, (t0, t1) in enumerate(HALVES[full]):
                    act.wait_ge(sem("p3_turned"), 2 * c + k + 1)
                    nc.scalar.activation(hs_write(hbz, c, full, 0, H)[:, t0:t1], tiles(bank(6 + k, (t1 - t0) * H, P), H),
                                         ACT.Copy).then_inc(sem("p3_high"), 1)
            chunks(act, step3)

            h3T = wts[:, 0:2 * C]

            def step4(c, full):
                n = width(full)
                for m in range(2):
                    act.wait_ge(sem("p4_own"), 2 * c + m + 1)
                    if m == 0:
                        wait_past(act, "p4_turned", c)
                    nc.scalar.activation(h3T[:, m * C:m * C + n], bank(2 + m, n), ACT.Copy).then_inc(sem("p4_ownT"), 1)
                for m in range(2):
                    act.wait_ge(sem("p4_h4"), 2 * c + m + 1)
                    nc.scalar.activation(actT[:, m * C:m * C + n], bank(4 + m, n), ACT.Relu, bias=bl1c[:, m:m + 1]).then_inc(sem("p4_relu"), 1)
                for m in range(2):
                    act.wait_ge(sem("p4_lin1"), 2 * c + m + 1)
                    nc.scalar.activation(aggT[:, m * C:m * C + n], bank(6 + m, n), ACT.Relu, bias=bac[:, m:m + 1]).then_inc(sem("p4_relu2"), 1)
                act.wait_ge(sem("p4_lin2"), c + 1)
                nc.scalar.activation(h3T[:, 0:n], bank(2, n), ACT.Identity, bias=bbc).then_inc(sem("p4_lin2T"), 1)
            chunks(act, step4)

        def pe_layers(pe, slow):
            def aggregate(acc, hs, w, h, c, full, s):
                n = width(full)
                for part in range(2):
                    last = nc.tensor.matmul(acc[:, 0:n], hs[:, ds(s * (2 * w) + part * w + h * 128, 128)],
                                            adj[0:P, ds(s * N + c * C, n)],
                                            start=(isinstance(s, int) and s == 0 and part == 0),
                                            stop=(isinstance(s, int) and s == S - 1 and part == 1), skip_group_check=True)
                return last

            def own(hs, w, h, b, c, full):
                for t in range(width(full) // P):
                    for part in range(2):
                        last = nc.tensor.matmul(bank(b)[:, t * P:(t + 1) * P],
                                                hs[:, ds((c * 4 + t) * (2 * w) + part * w + h * 128, 128)],
                                                identh[0:P, 0:P], start=(part == 0), stop=(part == 1))
                return last

            def dense(b, n, terms):
                for k, (wt, v) in enumerate(terms):
                    last = nc.tensor.matmul(bank(b, n), wt, v, start=(k == 0), stop=(k == len(terms) - 1))
                return last

            if slow:
                pe.wait_ge(sem("slow_consts"), 3)

                def degrees(c, full):
                    wait_past(pe, "sd_inv", c)
                    pe_slow(pe, 0, c, full, [bank(2, width(full))], 0).then_inc(sem("p0_agg"), 1)
                chunks(pe, degrees)

            def count(g, k, c_full, wait):
                pe.wait_ge(sem("onehot"), g + 1)
                wait_past(pe, "evicted", wait)
                for w in range(GW if c_full else 1):
                    last = nc.tensor.matmul(bank(k)[:, w * WD * S:(w + 1) * WD * S], ohp[k][:, :, w],
                                            ohn[k][:, 0:WD * S, w], start=True, stop=True)
                last.then_inc(sem("counted"), 1)

            def own1(c, full):
                wait_past(pe, "p1_zT", c)
                own(ha, D, 0, 6, c, full).then_inc(sem("p1_own"), 1)

            def hidden1(c, full):
                n = width(full)
                wait_past(pe, "p1_relu", 2 * c)
                pe.wait_ge(sem("p1_h0T"), c + 1)
                pe.wait_ge(sem("p1_agg_out"), c + 1)
                for m in range(2):
                    dense(4 + m, n, [(w1v[:, 0, m * 128:m * 128 + 128], aggT[:, C:C + n]),
                                     (w1v[:, 1, m * 128:m * 128 + 128], aggT[:, 0:n])]).then_inc(sem("p1_h1"), 1)

            def second1(c, full):
                n = width(full)
                pe.wait_ge(sem("p1_relu"), 2 * c + 2)
                dense(6, n, [(w2v[:, 2 + m, :], actT[:, m * C:m * C + n]) for m in range(2)]).then_inc(sem("p1_zm"), 1)
                wait_past(pe, "p1_self", c)
                dense(7, n, [(w2v[:, m, :], actT[:, m * C:m * C + n]) for m in range(2)]).then_inc(sem("p1_selfs"), 1)

            def turn1(c, full):
                pe.wait_ge(sem("p1_zT"), c + 1)
                wait_past(pe, "p1_low", c)
                for t in range(width(full) // P):
                    last = nc.tensor.transpose(bank(3, 4 * D, P)[:, t * D:(t + 1) * D], zT[:, t * P:(t + 1) * P], identf[:])
                last.then_inc(sem("p1_turned"), 1)

            def slow1(c, full):
                wait_past(pe, "p1_agg_out", c)
                pe_slow(pe, 1, c, full, [bank(2, width(full))], D).then_inc(sem("p1_agg"), 1)
                for part in (own1, hidden1, second1, turn1):
                    part(c, full)

            def step1(c, full, nxt, first=False):
                acc = bank(2)
                g = (c + 1) * S

                def piece(i):
                    if nxt is not None:
                        count(g + i, i % 2, nxt, g + i - 1)
                    return aggregate(acc, ha, D, 0, c, full, i)

                def pieces(a, b):
                    with pe.Fori(a // 2, b // 2) as h:
                        for k in (1, 2):
                            if nxt is not None:
                                count(g + 2 * h + k, k % 2, nxt, g + 2 * h + k - 1)
                            aggregate(acc, ha, D, 0, c, full, 2 * h + k)
                if not first:
                    own1(c - 1, True)
                if nxt is not None:
                    count(g, 0, nxt, g)
                pe.wait_ge(sem("evicted"), g)
                wait_past(pe, "p1_agg_out", c)
                aggregate(acc, ha, D, 0, c, full, 0)
                pieces(0, CUT1)
                if not first:
                    hidden1(c - 1, True)
                pieces(CUT1, CUT2)
                if not first:
                    second1(c - 1, True)
                pieces(CUT2, S - 3)
                piece(S - 2)
                piece(S - 1).then_inc(sem("p1_agg"), 1)
                if not first:
                    turn1(c - 1, True)

            pe.wait_ge(sem("n_low"), 1)
            pe.wait_ge(sem("w1_scaled"), 1)
            if slow:
                pe.wait_ge(sem("p1_rows"), 16)
                chunks(pe, slow1)
            else:
                for i in range(3):
                    count(i, i % 2, True, i - 1)
                with pe.Fori(1, (S - 1) // 2) as h:
                    for k in (1, 2):
                        count(2 * h + k, k % 2, True, 2 * h + k - 1)
                step1(0, True, True, first=True)
                with pe.Fori(1, NFULL - 1) as c:
                    step1(c, True, True)
                step1(NFULL - 1, True, False)
                step1(NFULL, False, None)
                for part in (own1, hidden1, second1, turn1):
                    part(NFULL, False)

            def staged(ph, aggs, parts):
                def slow_step(c, full):
                    wait_past(pe, f"p{ph}_agg_out", len(aggs) * c)
                    pe_slow(pe, ph, c, full, [a[0][:, 0:width(full)] for a in aggs], aggs[0][2]).then_inc(
                        sem(f"p{ph}_agg"), len(aggs))
                    for p in parts:
                        p(c, full)
                if slow:
                    chunks(pe, slow_step)
                    return

                def step(c, full, before):
                    if before is not None:
                        parts[0](c - 1, before)
                    wait_past(pe, f"p{ph}_agg_out", len(aggs) * c)
                    pieces = [(h, s) for h in range(len(aggs)) for s in range(S)]
                    npart = len(parts)
                    ends = [len(pieces) * (k + 1) // npart for k in range(npart)]
                    at = 0
                    for k in range(npart):
                        for h, s in pieces[at:ends[k]]:
                            acc, hs, w, hh = aggs[h]
                            last = aggregate(acc, hs, w, hh, c, full, s)
                            if s == S - 1:
                                last.then_inc(sem(f"p{ph}_agg"), 1)
                        at = ends[k]
                        if before is not None and k + 1 < npart:
                            parts[k + 1](c - 1, before)
                step(0, True, None)
                with pe.Fori(1, NFULL) as c:
                    step(c, True, True)
                step(NFULL, False, True)
                for p in parts:
                    p(NFULL, False)

            pe.wait_ge(sem("p1_low"), NCH)
            if slow:
                pe.wait_ge(sem("p2_rows"), 16)

            def nothing(c, full):
                pass

            def turn2(c, full):
                pe.wait_ge(sem("p2_sum"), c + 1)
                wait_past(pe, "p2_shifted", c)
                for t in range(width(full) // P):
                    last = nc.tensor.transpose(bank(3, 4 * D, P)[:, t * D:(t + 1) * D], aggT[:, t * P:(t + 1) * P], identf[:])
                last.then_inc(sem("p2_turned"), 1)
            staged(2, [(bank(2), hbz, D, 0)], [nothing, turn2])

            pe.wait_ge(sem("p2_low"), NCH)
            pe.wait_ge(sem("w0_in"), 16)
            if slow:
                pe.wait_ge(sem("p3_rows"), 16)

            def own3(c, full):
                wait_past(pe, "p3_ownT", c)
                own(ha, D, 0, 3, c, full).then_inc(sem("p3_own"), 1)

            def hidden3(c, full):
                n = width(full)
                pe.wait_ge(sem("p3_ownT"), c + 1)
                pe.wait_ge(sem("p3_agg_out"), c + 1)
                wait_past(pe, "p3_relu", 2 * c)
                for m in range(2):
                    dense(4 + m, n, [(wts[:, 256 + m * 128:384 + m * 128], aggT[:, C:C + n]),
                                     (wts[:, m * 128:m * 128 + 128], aggT[:, 0:n])]).then_inc(sem("p3_h3"), 1)

            def turn3(c, full):
                pe.wait_ge(sem("p3_relu"), 2 * c + 2)
                wait_past(pe, "p3_low", 2 * c)
                for k, (t0, t1) in enumerate(HALVES[full]):
                    for t in range(t0, t1):
                        for m in range(2):
                            at = ((t - t0) * 2 + m) * 128
                            last = nc.tensor.transpose(bank(6 + k, 4 * D, P)[:, at:at + 128],
                                                       actT[:, m * C + t * P:m * C + (t + 1) * P], identf[:])
                    last.then_inc(sem("p3_turned"), 1)
            staged(3, [(bank(2), ha, D, 0)], [own3, hidden3, turn3])

            l1v = w4[:, 0:512].rearrange("p (k o) -> p k o", k=2)
            r1v = w4[:, 512:1024].rearrange("p (k o) -> p k o", k=2)
            av = w4[:, 1024:1536].rearrange("p (k o) -> p k o", k=2)
            bv = w4[:, 1536:1792].rearrange("p (k o) -> p k o", k=2)
            h3T = wts[:, 0:2 * C]
            pe.wait_ge(sem("p3_low"), 2 * NCH - 1)
            if slow:
                pe.wait_ge(sem("p4_rows"), 16)

            def own4(c, full):
                wait_past(pe, "p4_lin2T", c)
                own(hbz, H, 0, 2, c, full).then_inc(sem("p4_own"), 1)
                wait_past(pe, "p4_sum", c)
                own(hbz, H, 1, 3, c, full).then_inc(sem("p4_own"), 1)

            def hidden4(c, full):
                n = width(full)
                pe.wait_ge(sem("w4_in"), 16)
                pe.wait_ge(sem("p4_ownT"), 2 * c + 2)
                pe.wait_ge(sem("p4_agg_out"), 2 * c + 2)
                wait_past(pe, "p4_relu", 2 * c)
                for m in range(2):
                    o = slice(m * 128, m * 128 + 128)
                    dense(4 + m, n, [(r1v[:, 0, o], h3T[:, 0:n]), (r1v[:, 1, o], h3T[:, C:C + n]),
                                     (l1v[:, 0, o], aggT[:, 0:n]), (l1v[:, 1, o], aggT[:, C:C + n])]).then_inc(sem("p4_h4"), 1)

            def lin1(c, full):
                n = width(full)
                pe.wait_ge(sem("p4_relu"), 2 * c + 2)
                wait_past(pe, "p4_relu2", 2 * c)
                for m in range(2):
                    o = slice(m * 128, m * 128 + 128)
                    dense(6 + m, n, [(av[:, k, o], actT[:, k * C:k * C + n]) for k in range(2)]).then_inc(sem("p4_lin1"), 1)

            def lin2(c, full):
                n = width(full)
                pe.wait_ge(sem("p4_relu2"), 2 * c + 2)
                dense(2, n, [(bv[:, k, :], aggT[:, k * C:k * C + n]) for k in range(2)]).then_inc(sem("p4_lin2"), 1)

            def turn4(c, full):
                pe.wait_ge(sem("p4_lin2T"), c + 1)
                for t in range(width(full) // P):
                    last = nc.tensor.transpose(bank(3, 4 * D, P)[:, t * D:(t + 1) * D], h3T[:, t * P:(t + 1) * P], identf[:])
                last.then_inc(sem("p4_turned"), 1)
            staged(4, [(bank(0), hbz, H, 0), (bank(1), hbz, H, 1)], [own4, hidden4, lin1, lin2, turn4])

        @block.sync
        def _(sp):
            sp.dma_start(dst_i, dst.rearrange("(r e) -> r e", r=ER)).then_inc(sem("dst_in"), 16)
            sp.dma_start(src_i, src.rearrange("(r e) -> r e", r=ER)).then_inc(sem("src_in"), 16)
            sp.dma_start(tiles(xs0, D), x.rearrange("(t p) d -> p t d", p=P)).then_inc(sem("x_in"), 16)
            n = 0
            for name, w in (("l0", Wl0), ("r0", Wr0), ("l1", Wl1), ("r1", Wr1), ("a", Wa), ("b", Wb)):
                at, kt, mt = WN[name]
                sp.dma_start(wn[:, at:at + kt * mt * 128].rearrange("p (m k) -> p m k", m=mt),
                             w.rearrange("(m p) k -> p m k", p=128)).then_inc(sem("w_in"), 16)
                n += 1
            sp.dma_start(w1v, W1.rearrange("(k p) o -> p k o", p=128)).then_inc(sem("w_in"), 16)
            sp.dma_start(w2v, W2.rearrange("(k p) o -> p k o", p=128)).then_inc(sem("w_in"), 16)
            for dstc, b, k in ((b1c, b1, 2), (bl0c, bl0, 2), (bl1c, bl1, 2), (bac, ba, 2), (b2c, b2, 1), (bbc, bb, 1)):
                with nc.allow_non_contiguous_dma(reason="one bias per partition"):
                    sp.dma_start(dstc, b.rearrange("(k p) -> p k", k=k)).then_inc(sem("w_in"), 16)
            sp.wait_ge(sem("keys"), 1)
            sp.dma_start(key_d[0:E].rearrange("(r e) -> r e", r=ER), keyf).then_inc(sem("key_out"), 16)
            sp.wait_ge(sem("padk"), 1)
            sp.dma_start(key_d[E:E + 250].rearrange("(o e) -> o e", o=1), padk[0:1, 0:250]).then_inc(sem("key_out"), 16)
            sp.wait_ge(sem("wt"), 5)
            sp.dma_start(wt_d, wt_s).then_inc(sem("wt_out"), 16)
            branch(sp, sp_layers)

        @block.gpsimd
        def _(pool):
            nc.gpsimd.memset(identf[:], 0.0).then_inc(sem("pool"), 1)
            nc.gpsimd.memset(identh[:], 0.0).then_inc(sem("pool"), 1)
            nc.gpsimd.memset(padk[:, :], 1.2e7).then_inc(sem("padk"), 1)
            nc.gpsimd.memset(onesf[:, :], 1.0).then_inc(sem("ones"), 1)
            nc.gpsimd.memset(ones_c, 1.0).then_inc(sem("ones"), 1)
            nc.gpsimd.memset(epsc, 1e-5).then_inc(sem("ones"), 1)
            pool.wait_ge(sem("pool"), 2)
            for t in (identf, identh):
                nc.gpsimd.affine_select(out=t[:], in_=t[:], compare_op=ALU.not_equal, fill=1.0, base=0,
                                        pattern=[[-1, 128]], channel_multiplier=1).then_inc(sem("ident"), 1)
            nc.gpsimd.iota(thr, [[WD * P, QG]], base=0, channel_multiplier=WD,
                           allow_small_or_imprecise_dtypes=True).then_inc(sem("iota"), 1)
            nc.gpsimd.iota(iota4, [[1, 128], [0, GW]], base=0, channel_multiplier=0,
                           allow_small_or_imprecise_dtypes=True).then_inc(sem("iota"), 1)
            pool.wait_ge(sem("rowi"), 1)
            pool.wait_ge(sem("key_out"), 32)
            for g in range(QG):
                pool.indirect_dma_start(rows[:, g * EC:(g + 1) * EC], None,
                                        key_d[0:E].rearrange("(r e) -> r e", e=EC),
                                        bass.IndirectOffsetOnAxis(rowi[:, g:g + 1], 0)).then_inc(sem(f"rows{g}"), 16)
            pool.wait_ge(sem("starti"), 1)
            for g in range(QG):
                pool.indirect_dma_start(gk[:, g * CAP:(g + 1) * CAP], None,
                                        key_d.rearrange("(e o) -> e o", o=1),
                                        bass.IndirectOffsetOnAxis(starti[:, g:g + 1], 0)).then_inc(sem(f"gk{g}"), 16)
            branch(pool, pool_layers)

        @block.vector
        def _(dve):
            lk = Link(dve, "dve")
            dve.wait_ge(sem("dst_in"), 16)
            nc.vector.tensor_copy(dstf, dst_i).then_inc(sem("dstf"), 1)
            dve.wait_ge(sem("src_in"), 16)
            lk(nc.vector.tensor_scalar(t_i, src_i, float(DIV_M), None, ALU.mult))
            lk(nc.vector.tensor_scalar(s_i, t_i, DIV_S, None, ALU.logical_shift_right))
            dve.wait_ge(sem("dstf"), 1)
            lk(nc.vector.scalar_tensor_tensor(keyf, dstf, float(S * KEY), src_i, ALU.mult, ALU.add))
            nc.vector.scalar_tensor_tensor(keyf, s_i, float(KEY - P), keyf, ALU.mult, ALU.add).then_inc(sem("keys"), 1)
            dve.wait_ge(sem("ident"), 2)
            nc.vector.tensor_scalar(diag, identf[0:ER, 0:ER], dstf[:, 0:1], None, ALU.mult).then_inc(sem("diag"), 1)
            dve.wait_ge(sem("iota"), 2)
            dve.wait_ge(sem("firsts"), 1)
            for g in range(QG):
                last = nc.vector.tensor_scalar(scr[0:P, 0:ER], bank(0, ER, P), thr[:, g:g + 1], None, ALU.is_lt, ALU.add,
                                               accum_out=rowf[:, g:g + 1])
                lk(last)
            lk(nc.vector.tensor_scalar(rowf, rowf, -1.0, 0.0, ALU.add, ALU.max))
            nc.vector.tensor_copy(rowi, rowf).then_inc(sem("rowi"), 1)
            lk(nc.vector.tensor_scalar(wbase, thr, float(S * KEY), None, ALU.mult))
            dve.wait_ge(sem("x_in"), 16)

            def starts():
                for g in range(QG):
                    dve.wait_ge(sem(f"rows{g}"), 16)
                    lk(nc.vector.tensor_scalar(scr[0:P, 0:EC], rows[:, g * EC:(g + 1) * EC], wbase[:, g:g + 1], None,
                                               ALU.is_lt, ALU.add, accum_out=cnt[:, g:g + 1]))
                lk(nc.vector.scalar_tensor_tensor(rowf, rowf, float(EC), cnt[:, 0:QG], ALU.mult, ALU.add))
                nc.vector.tensor_copy(starti, rowf).then_inc(sem("starti"), 1)
            ln_dve(dve, lk, "n_", 1, xs0, xc0, sq0, st0, S, h0v[:, :, 0, :], h0v[:, :, 1, :], before=starts)
            for g in range(QG):
                dve.wait_ge(sem(f"gk{g}"), 16)
                v = gk[:, g * CAP:(g + 1) * CAP]
                nc.vector.tensor_scalar(v, v, wbase[:, g:g + 1], None, ALU.subtract).then_inc(sem("relative"), 1)
            dve.wait_ge(sem("relative"), QG)
            c3 = cnt[:, 0:(WD + 1) * QG].rearrange("p (g j) -> p g j", j=WD + 1)
            for g in range(QG):
                for j in range(WD + 1):
                    last = nc.vector.tensor_scalar(scr[0:P, 0:CAP], gk[:, g * CAP:(g + 1) * CAP], float(j * S * KEY), None,
                                                   ALU.is_lt, ALU.add, accum_out=c3[:, g, j:j + 1])
                    lk(last)
            d3 = deg.rearrange("p (g j) -> p g j", j=WD)
            lk(nc.vector.tensor_tensor(d3, c3[:, :, 1:WD + 1], c3[:, :, 0:WD], ALU.subtract))
            nc.vector.tensor_reduce(flag_f[0:P], deg, AX, ALU.add).then_inc(sem("held"), 1)
            lk(nc.vector.tensor_scalar(deg, deg, 1.0, None, ALU.max))
            nc.vector.reciprocal(deg, deg).then_inc(sem("inverse"), 1)
            dve.wait_ge(sem("held_sum"), 1)
            nc.vector.tensor_scalar(flag_i[0:1], bank(1, 1, 1), float(E), None, ALU.is_equal).then_inc(sem("flag"), 1)
            dve.wait_ge(sem("keysT"), 1)
            lk(nc.vector.tensor_copy(k_i[:, 0:4 * P], bank(2, 4 * P)))
            lk(nc.vector.tensor_copy(k_i[:, 4 * P:NWIN], bank(3, P)))
            lk(nc.vector.tensor_scalar(kp_i, k_i, KEY - 1, None, ALU.bitwise_and))
            lk(nc.vector.tensor_copy(kp[:, :], kp_i))
            lk(nc.vector.tensor_scalar(k_i, k_i, 7, None, ALU.arith_shift_right))
            lk(nc.vector.tensor_scalar(kn[:, :], k_i, 200.0, -1.0, ALU.min, ALU.max))
            dve.wait_ge(sem("w_in"), 16 * NW)
            wa = scr[:, 0:512]
            lk(nc.vector.tensor_reduce(bnd, wn[:, 0:256].rearrange("p (m k) -> p m k", m=2), AX, ALU.add, apply_absolute_value=True))
            lk(nc.vector.tensor_reduce(tmp2, wn[:, 256:512].rearrange("p (m k) -> p m k", m=2), AX, ALU.add, apply_absolute_value=True))
            lk(nc.vector.tensor_tensor(bnd, bnd, tmp2, ALU.add))
            lk(absolute(tmp2, bl0c))
            lk(nc.vector.scalar_tensor_tensor(bnd, bnd, LN_BOUND, tmp2, ALU.mult, ALU.add))

            def pow2(scale, inverse, bound):
                lk(nc.vector.tensor_scalar(bound, bound, 1e-20, None, ALU.max))
                lk(nc.vector.reciprocal(bound, bound))
                lk(nc.vector.tensor_scalar(bound, bound, TOP, None, ALU.mult))
                lk(nc.vector.tensor_scalar(scale.bitcast(I32), bound.bitcast(I32), EXP_MASK, None, ALU.bitwise_and))
                lk(nc.vector.tensor_scalar(inverse.bitcast(I32), scale.bitcast(I32), -1.0, float(EXP_FLIP), ALU.mult, ALU.add))
            pow2(s3, is3, bnd)
            lk(nc.vector.tensor_tensor(b3s, bl0c, s3, ALU.mult))
            nc.vector.tensor_copy(tmp3, is3).then_inc(sem("scale3"), 1)
            lk(absolute(wa, wts[:, 0:512]))
            absolute(scr[:, 512:768], wts[:, 768:1024]).then_inc(sem("absw"), 1)
            lk(absolute(tmp2, b1c))
            dve.wait_ge(sem("bound1"), 1)
            nc.vector.scalar_tensor_tensor(bnd, bank(0, 2), LN_BOUND, tmp2, ALU.mult, ALU.add).then_inc(sem("bound1s"), 1)
            dve.wait_ge(sem("boundz"), 1)
            lk(nc.vector.tensor_copy(bndz, bank(0, 3)[:, 2:3]))
            pow2(zs, izs, bndz)
            nc.vector.tensor_scalar(wts[:, 0:512], wts[:, 0:512], 1.0 / LN_SCALE, None, ALU.mult).then_inc(sem("w1_scaled"), 1)
            branch(dve, dve_layers)

        @block.scalar
        def _(act):
            act.wait_ge(sem("ones"), 3)
            ln_act(act, "n_", 1, xc0, sq0, st0, S, h0v[:, :, 0, :])
            act.wait_ge(sem("scale3"), 1)
            for k in range(5):
                act.wait_ge(sem("wturned"), k + 1)
                if k == 0:
                    nc.scalar.activation(wt_s[:, 0:512], bank(4), ACT.Copy, scale=1.0 / LN_SCALE).then_inc(sem("wt"), 1)
                elif k < 3:
                    for kt in range(2):
                        last = nc.scalar.activation(wt_s[:, 512 * k + 256 * kt:512 * k + 256 * kt + 256],
                                                    bank(4 + k % 2)[:, 256 * kt:256 * kt + 256], ACT.Identity, scale=is3[:, kt:kt + 1])
                    last.then_inc(sem("wt"), 1)
                else:
                    n = 512 if k == 3 else 256
                    nc.scalar.activation(wt_s[:, 512 * k:512 * k + n], bank(4 + k % 2, n), ACT.Copy).then_inc(sem("wt"), 1)
            branch(act, act_layers)

        @block.tensor
        def _(pe):
            pe.wait_ge(sem("ones"), 3)
            pe.wait_ge(sem("ident"), 2)
            pe.wait_ge(sem("diag"), 1)
            nc.tensor.matmul(bank(0, ER, P), onesf[0:ER, 0:P], diag, start=True, stop=True).then_inc(sem("firsts"), 1)
            pe.wait_ge(sem("relative"), QG)
            for g in range(QG):
                at = 2 * BANK + g * P if g < 4 else 3 * BANK
                last = nc.tensor.transpose(ps[:, at:at + P], gk[:, g * CAP:(g + 1) * CAP], identf[0:P, 0:P])
            last.then_inc(sem("keysT"), 1)
            pe.wait_ge(sem("held"), 1)
            nc.tensor.matmul(bank(1, 1, 1), flag_f[0:P], onesf[0:P, 0:1], start=True, stop=True).then_inc(sem("held_sum"), 1)
            pe.wait_ge(sem("w_in"), 16 * NW)
            blocks = []
            for name in ("l0", "r0", "l1", "r1", "a", "b"):
                at, kt, mt = WN[name]
                for k in range(kt):
                    for m in range(mt):
                        blocks.append(wn[:, at + (m * kt + k) * 128:at + (m * kt + k) * 128 + 128])
            for n, b in enumerate(blocks):
                if n % 4 == 0 and n >= 8:
                    pe.wait_ge(sem("wt"), n // 4 - 1)
                last = nc.tensor.transpose(bank(4 + (n // 4) % 2)[:, (n % 4) * 128:(n % 4) * 128 + 128], b, identf[:])
                if n % 4 == 3 or n == len(blocks) - 1:
                    last.then_inc(sem("wturned"), 1)
            pe.wait_ge(sem("absw"), 1)
            for m in range(2):
                for k in range(2):
                    last = nc.tensor.matmul(bank(0)[:, m:m + 1], scr[:, k * 256 + m * 128:k * 256 + m * 128 + 128], ones_c,
                                            start=(k == 0), stop=(k == 1))
            last.then_inc(sem("bound1"), 1)
            pe.wait_ge(sem("bound1s"), 1)
            for m in range(2):
                last = nc.tensor.matmul(bank(0)[:, 2:3], scr[:, 512 + m * 128:640 + m * 128], bnd[:, m:m + 1],
                                        start=(m == 0), stop=(m == 1))
            last.then_inc(sem("boundz"), 1)
            branch(pe, pe_layers)


_INS = ["x", "src", "dst", "L0_gnn_W1", "L0_gnn_b1", "L0_gnn_W2", "L0_gnn_b2", "L1_gnn_W_l0", "L1_gnn_b_l0", "L1_gnn_W_r0",
        "L1_gnn_W_l1", "L1_gnn_b_l1", "L1_gnn_W_r1", "L1_gnn_W_lin1", "L1_gnn_b_lin1", "L1_gnn_W_lin2", "L1_gnn_b_lin2"]


def kernel(**inputs):
    import numpy as _np
    import concourse.bacc as _bacc
    from concourse import mybir as _mybir
    from concourse.bass_utils import run_bass_kernel_spmd as _run

    nc = _bacc.Bacc("TRN2", target_bir_lowering=False, num_devices=1)
    arrays, args = {}, []
    for name in _INS:
        a = _np.ascontiguousarray(inputs[name])
        arrays[f"in_{name}_dram"] = a
        args.append(nc.dram_tensor(f"in_{name}_dram", a.shape, _mybir.dt.from_np(a.dtype), kind="ExternalInput").ap())
    out = nc.dram_tensor("out_0_dram", (N, D), _mybir.dt.float32, kind="ExternalOutput").ap()
    sage_program(nc, *args, out)
    r = _run(nc, [arrays], core_ids=[0])
    return r.results[0]["out_0_dram"]
```

```python
from contextlib import ExitStack

import concourse.bass as bass
from concourse import mybir

F32 = mybir.dt.float32
F16 = mybir.dt.float16
I32 = mybir.dt.int32
ALU = mybir.AluOpType
ACT = mybir.ActivationFunctionType
AX = mybir.AxisListType.X
ds = bass.ds

N = 3125
E = 50000
D = 128
H = 256
P = 125
S = N // P
ER = 125
EC = E // ER

WD = 5
NWIN = N // WD
KEY = 128
CAP = 128
GW = 4
QG = NWIN // P
DIV_M, DIV_S = 4195, 19

C = 500
NFULL = N // C
NCH = NFULL + 1
BANK = 512
NW = 14
HALVES = {True: ((0, 2), (2, 4)), False: ((0, 1),)}
LN_SCALE = 4096.0
LN_BOUND = 11.5
TOP = 32768.0
SLOT0 = 3
XA = 10
CUT1, CUT2 = 6, 12
EXP_MASK = 0x7F800000
EXP_FLIP = 254 << 23


def width(full):
    return C if full else N - NFULL * C


def sage_program(nc, x, src, dst, W1, b1, W2, b2, Wl0, bl0, Wr0, Wl1, bl1, Wr1, Wa, ba, Wb, bb, out):
    ctx = ExitStack()
    with ctx:
        def sb(name, cols, dt=F32):
            return ctx.enter_context(nc.sbuf_tensor(name, [128, cols], dt))

        sems = {}

        def sem(name):
            if name not in sems:
                sems[name] = ctx.enter_context(nc.semaphore(name))
            return sems[name]

        def over(t, at, cols, dt):
            n = cols * (2 if dt == F16 else 4) // 2
            v = t[:, at // 2:at // 2 + n]
            return v if dt == F16 else v.bitcast(dt)

        key_d = nc.dram_tensor("key_d", [E + ER * 2], F32, kind="Internal").ap()
        inv_d = nc.dram_tensor("inv_d", [N], F32, kind="Internal").ap()
        wt_d = nc.dram_tensor("wt_d", [128, 2304], F32, kind="Internal").ap()
        self_d = nc.dram_tensor("self_d", [128, N], F32, kind="Internal").ap()
        x1_d = nc.dram_tensor("x1_d", [N, D], F32, kind="Internal").ap()
        hs_d1 = nc.dram_tensor("hs_d1", [N, 2 * D], F16, kind="Internal").ap()
        hs_d2 = nc.dram_tensor("hs_d2", [N, 2 * D], F16, kind="Internal").ap()
        hs_d3 = nc.dram_tensor("hs_d3", [N, 2 * D], F16, kind="Internal").ap()
        hs_d4 = nc.dram_tensor("hs_d4", [N, 2 * H], F16, kind="Internal").ap()

        adj = sb("adj", S * N + 1, F16)
        hs_a = sb("hs_a", S * 2 * D, F16)
        hs_b = sb("hs_b", S * 2 * H, F16)
        wts = sb("wts", 1024)
        invc = sb("invc", C)
        aggT = sb("aggT", 2 * C)
        actT = sb("actT", 2 * C)
        zT = sb("zT", C)
        identf = sb("identf", 128)
        identh = sb("identh", 128, F16)
        st = sb("st", 24)
        iota = sb("iota", P * GW, F16)
        col = sb("col", 40)
        ps = ctx.enter_context(nc.psum_tensor("ps", [128, 8 * BANK], F32))

        def bank(i, cols=BANK, rows=128):
            return ps[0:rows, i * BANK:i * BANK + cols]

        def acc3(c, slow):
            return 1 if isinstance(c, int) and c == 1 and not slow else 2

        b1c, b2c, bl0c, bl1c, bac, bbc = (col[:, 0:2], col[:, 2:3], col[:, 3:5], col[:, 5:7], col[:, 7:9], col[:, 9:10])
        s3, is3, b3s = col[:, 10:12], col[:, 12:14], col[:, 14:16]
        zs, izs = col[:, 16:17], col[:, 17:18]
        bnd = col[:, 18:20]
        tmp2 = col[:, 20:22]
        ones_h = col[:, 22:23].bitcast(F16)[:, 0:1]
        held = col[:, 36:38]
        bl0a = col[:, 32:34]
        b1a = col[:, 34:36]
        ones_c = col[:, 23:24]
        flag_f = col[:, 24:25]
        flag_i = col[:, 25:26].bitcast(I32)
        bndz = col[:, 26:27]
        mhalf = col[:, 28:32]

        o = [0]

        def lay(cols, dt):
            at = o[0]
            o[0] += (cols * (2 if dt == F16 else 4) + 63) // 64 * 64
            return over(adj, at, cols, dt)
        dst_i, src_i, t_i, s_i = (lay(EC, I32)[0:ER] for _ in range(4))
        dstf, keyf, dstrel = (lay(EC, F32)[0:ER] for _ in range(3))
        rows = lay(QG * EC, F32)[0:P]
        junk = [lay(128, F32)[0:P] for _ in range(QG)]
        absw = lay(768, F32)
        wn = lay(2304, F32)
        wt_s = lay(2304, F32)
        thr = lay(QG, F32)[0:P]
        wbase = lay(QG, F32)[0:P]
        inrow = lay(QG, F32)[0:P]
        gk = lay(QG * CAP, F32)[0:P]
        rowi = lay(QG, I32)[0:P]
        rowf = lay(QG, F32)[0:P]
        starti = lay(QG, I32)[0:P]
        diag = lay(ER, F32)[0:ER]
        onesf = lay(128, F32)
        bns0 = lay(S * 6, F32)[0:P]
        mv0 = lay(S * 2, F32)[0:P]
        var0, nmean0, rstd0, nmr0, mhalf0 = (lay(S, F32)[0:P] for _ in range(5))
        k_i = lay(NWIN, I32)
        kp_i = lay(NWIN, I32)
        kn_i = lay(NWIN, I32)
        padk = lay(256, F32)
        iota5 = lay(C, F16)[0:ER]
        zeros = lay(C, F16)[0:ER]
        onesh = lay(128, F16)[0:ER]
        oh = lay(C, F16)[0:ER]
        gbuf = lay(2 * H, F16)[0:ER]
        idx = lay(1, I32)[0:ER]
        assert o[0] <= S * N * 2
        below = [t[:, :].bitcast(F16)[:, k * NWIN:(k + 1) * NWIN] for t in (aggT, actT) for k in range(3)]
        assert len(below) == WD + 1 and 3 * NWIN <= 4 * C
        deg = zT[0:P, 0:QG * WD]
        cnt = zT[0:P, QG * WD:QG * (2 * WD + 1)]
        xs0 = over(hs_b, 0, S * D, F32)[0:P]
        up = S * 2 * D * 2
        kpn = over(hs_b, up, 2 * NWIN, F16)
        kp, kn = kpn[:, 0:NWIN], kpn[:, NWIN:]
        keys = kpn.rearrange("p (k n) -> p k n", k=2)
        by_window = lambda t: t.rearrange("p (v w) -> p v w", w=GW)
        onehots = [over(hs_b, up + 2560 + 2048 * i, 2 * P * GW, F16).rearrange("p (k v w) -> p k v w", k=2, w=GW)
                   for i in range(4)]
        iota4 = by_window(iota)
        selfT = over(hs_b, up + 10752, C, F32)
        xin, yc, sqb, x1b = (over(hs_b, up + 2048 * i, 4 * D, F32)[0:P] for i in range(4))
        selfc = over(hs_b, up + 8192, C, F32)
        bns = over(hs_b, up + 10240, 4 * 6, F32)[0:P]
        mv = over(hs_b, up + 10368, 4 * 2, F32)[0:P]
        w4 = over(hs_a, 0, 1792, F32)
        x1in = over(hs_a, 7168, 4 * D, F32)[0:P]
        outb = over(hs_a, 9216, 4 * D, F32)[0:P]

        w1v = wts[:, 0:512].rearrange("p (k o) -> p k o", k=2)
        w2v = wts[:, 512:1024].rearrange("p (k o) -> p k o", k=4)
        ha = hs_a[0:P]
        hbz = hs_b[0:P]

        def tiles(t, w):
            return t.rearrange("p (t d) -> p t d", d=w)

        def hs_write(h, c, full, part, w):
            n = width(full) // P
            v = h[:, ds(c * (4 * 2 * w), n * 2 * w)].rearrange("p (t k d) -> p t k d", k=2, d=w)
            return v[:, :, part, :]

        class Link:

            def __init__(self, eng, name, base=0):
                self.eng, self.sem, self.base, self.n = eng, sem(name), base, 0

            def __call__(self, ins):
                self.n += 1
                ins.then_inc(self.sem, 1)
                self.eng.wait_ge(self.sem, self.base + self.n)

        def wait_past(eng, name, value):
            if not isinstance(value, int) or value > 0:
                eng.wait_ge(sem(name), value)

        def chunks(eng, emit):
            emit(0, True)
            with eng.Fori(1, NFULL) as c:
                emit(c, True)
            emit(NFULL, False)

        def ln_stats(lk, X, XC, T, stats, mean_var, out_v, p, in_loop=False):
            for t in range(T):
                last = nc.vector.bn_stats(stats[:, 6 * t:6 * t + 6], X[:, t * D:(t + 1) * D])
            lk(last)
            if in_loop:
                lk.eng.sem_inc(sem(p + "stats_seen"), 1)
            for t in range(T):
                last = nc.vector.bn_aggr(mean_var[:, 2 * t:2 * t + 2], stats[:, 6 * t:6 * t + 6])
            lk(last)
            mv2 = tiles(mean_var[:, 0:2 * T], 2)
            nc.vector.tensor_scalar(out_v, mv2[:, :, 1], 1e-5, LN_SCALE ** -2, ALU.add, ALU.mult).then_inc(sem(p + "var"), 1)
            nc.vector.tensor_tensor(tiles(XC[:, 0:T * D], D), tiles(X[:, 0:T * D], D),
                                    mv2[:, :, 0:1].to_broadcast([P, T, D]), ALU.subtract).then_inc(sem(p + "centred"), 1)

        block = ctx.enter_context(nc.Block())

        h0v = ha.rearrange("p (t k d) -> p t k d", k=2, d=D)
        WN = {"l0": (0, 1, 2), "r0": (256, 1, 2), "l1": (512, 2, 2), "r1": (1024, 2, 2), "a": (1536, 2, 2), "b": (2048, 2, 1)}

        def sp_layers(sp, slow):
            if not slow:
                sp.wait_ge(sem("inverse"), 1)
                with nc.allow_non_contiguous_dma(reason="runs of 5 inverse degrees"):
                    sp.dma_start(inv_d.rearrange("(g q j) -> q g j", q=P, j=WD),
                                 deg.rearrange("q (g j) -> q g j", j=WD)).then_inc(sem("inv_out"), 16)
            else:
                def store_inv(c, full):
                    sp.wait_ge(sem("sd_inv"), c + 1)
                    sp.dma_start(inv_d[ds(c * C, width(full))].rearrange("(o e) -> o e", o=1),
                                 invc[0:1, 0:width(full)]).then_inc(sem("inv_out"), 16)
                    sp.wait_ge(sem("inv_out"), 16 * c + 16)
                    sp.sem_inc(sem("inv_out_seen"), 1)
                chunks(sp, store_inv)
            ninv = NCH if slow else 1
            sp.wait_ge(sem("inv_out"), 16 * ninv)

            def load_inv(p, c, full):
                sp.dma_start(invc[:, 0:width(full)],
                             inv_d[ds(c * C, width(full))].partition_broadcast(128)).then_inc(sem(p + "inv"), 16)

            def spread(ph, hs, w, hd):
                if slow:
                    sp.dma_start(hd.rearrange("(t p) f -> p t f", p=P),
                                 hs.rearrange("p (t f) -> p t f", f=2 * w)).then_inc(sem(f"p{ph}_rows"), 16)

            def each(emit):
                emit(0, True, True)
                with sp.Fori(1, NFULL - 1) as c:
                    emit(c, True, True)
                emit(NFULL - 1, True, False)
                emit(NFULL, False, None)

            sp.wait_ge(sem("n_low"), 1)
            spread(1, ha, D, hs_d1)
            load_inv("p1_", 0, True)

            def step1(c, full, nxt):
                sp.wait_ge(sem("p1_agg_out"), c + 1)
                if nxt is not None:
                    load_inv("p1_", c + 1, nxt)
                sp.wait_ge(sem("p1_self"), c + 1)
                sp.dma_start(self_d[:, ds(c * C, width(full))], selfT[:, 0:width(full)]).then_inc(sem("p1_self_out"), 16)
            each(step1)
            sp.wait_ge(sem("p1_h1"), 2 * NCH)
            sp.wait_ge(sem("wt_out"), 16)
            sp.dma_start(wts[:, 0:512], wt_d[:, 0:512]).then_inc(sem("w0_in"), 16)
            sp.wait_ge(sem("p1_self_out"), 16 * NCH)
            sp.wait_ge(sem("p1_low"), NCH)
            spread(2, hbz[:, 0:S * 2 * D], D, hs_d2)

            def load_self(c, full):
                sp.dma_start(selfc[:, 0:width(full)], self_d[:, ds(c * C, width(full))]).then_inc(sem("p2_self"), 16)

            def load_x(c, full):
                sp.dma_start(tiles(xin[:, 0:width(full) // P * D], D),
                             x[ds(c * C, width(full)), :].rearrange("(t p) d -> p t d", p=P)).then_inc(sem("p2_x"), 16)
            load_inv("p2_", 0, True)
            load_self(0, True)
            load_x(0, True)

            def step2(c, full, nxt):
                if nxt is not None:
                    sp.wait_ge(sem("p2_agg_out"), c + 1)
                    load_inv("p2_", c + 1, nxt)
                    sp.wait_ge(sem("p2_sum"), c + 1)
                    load_self(c + 1, nxt)
                    sp.wait_ge(sem("p2_x_used"), c + 1)
                    load_x(c + 1, nxt)
                sp.wait_ge(sem("p2_x1"), c + 1)
                sp.dma_start(x1_d[ds(c * C, width(full)), :].rearrange("(t p) d -> p t d", p=P),
                             tiles(x1b[:, 0:width(full) // P * D], D)).then_inc(sem("p2_x1_out"), 16)
            each(step2)
            sp.wait_ge(sem("p2_x1_out"), 16 * NCH)
            sp.wait_ge(sem("p2_low"), NCH)
            spread(3, ha, D, hs_d3)
            load_inv("p3_", 0, True)

            def step3(c, full, nxt):
                if nxt is not None:
                    sp.wait_ge(sem("p3_agg_out"), c + 1)
                    load_inv("p3_", c + 1, nxt)
            each(step3)
            sp.wait_ge(sem("p3_agg_out"), NCH)
            sp.wait_ge(sem("p3_own"), NCH)
            if slow:
                sp.wait_ge(sem("p3_rows"), 16)
            sp.dma_start(w4, wt_d[:, 512:2304]).then_inc(sem("w4_in"), 16)
            sp.wait_ge(sem("p3_low"), 2 * NCH - 1)
            spread(4, hbz, H, hs_d4)
            load_inv("p4_", 0, True)

            def load_x1(c, full):
                sp.dma_start(tiles(x1in[:, 0:width(full) // P * D], D),
                             x1_d[ds(c * C, width(full)), :].rearrange("(t p) d -> p t d", p=P)).then_inc(sem("p4_x1"), 16)
            load_x1(0, True)

            def step4(c, full, nxt):
                sp.wait_ge(sem("p4_agg_out"), 2 * c + 2)
                if nxt is not None:
                    load_inv("p4_", c + 1, nxt)
                sp.wait_ge(sem("p4_sum"), c + 1)
                sp.dma_start(out[ds(c * C, width(full)), :].rearrange("(t p) d -> p t d", p=P),
                             tiles(outb[:, 0:width(full) // P * D], D)).then_inc(sem("p4_out"), 16)
                if nxt is not None:
                    load_x1(c + 1, nxt)
            each(step4)
            sp.wait_ge(sem("p4_out"), 16 * NCH)

        def branch(eng, layers):
            eng.wait_ge(sem("flag"), 1)
            fits = eng.value_load(flag_i[0:1, 0:1], min_val=0, max_val=1)
            with eng.If(fits == 1):
                layers(eng, False)
            with eng.Else():
                layers(eng, True)

        def pool_layers(pool, slow):
            if slow:
                nc.gpsimd.iota(iota5, [[1, C]], base=0, channel_multiplier=0,
                               allow_small_or_imprecise_dtypes=True).then_inc(sem("slow_consts"), 1)
                nc.gpsimd.memset(zeros, 0.0).then_inc(sem("slow_consts"), 1)
                nc.gpsimd.memset(onesh, 1.0).then_inc(sem("slow_consts"), 1)

            def gathers(ph, hd, w, c):
                with pool.Fori(0, EC) as j:
                    u = c * EC + j
                    pool.wait_ge(sem(f"p{ph}_edge"), 2 * u + 2)
                    pool.sem_inc(sem(f"p{ph}_edge_seen"), 1)
                    pool.indirect_dma_start(gbuf[:, 0:2 * w], None, hd,
                                            bass.IndirectOffsetOnAxis(idx, 0)).then_inc(sem(f"p{ph}_gathered"), 16)

            def phase(ph, hd, w, emit):
                if slow:
                    pool.wait_ge(sem(f"p{ph}_rows"), 16)

                def step(c, full):
                    if slow:
                        gathers(ph, hd, w, c)
                    if emit:
                        emit(c, full)
                if slow or emit:
                    chunks(pool, step)

            pool.wait_ge(sem("mhalf"), 1)

            def rstd2(c, full):
                nt = width(full) // P
                pool.wait_ge(sem("p2_var"), c + 1)
                nc.gpsimd.tensor_tensor(st[0:P, 16:16 + nt], st[0:P, 12:12 + nt], mhalf[0:P, 0:nt], ALU.pow).then_inc(
                    sem("p2_rstd"), 1)
            phase(1, hs_d1, D, None)
            phase(2, hs_d2, D, rstd2)
            phase(3, hs_d3, D, None)
            phase(4, hs_d4, H, None)

        def dve_slow(dve, ph, c):
            with dve.Fori(0, EC) as j:
                u = c * EC + j
                dve.wait_ge(sem(f"p{ph}_edge_used"), u + 1)
                nc.vector.tensor_copy(idx, src_i[:, ds(j, 1)]).then_inc(sem(f"p{ph}_edge"), 1)
                nc.vector.tensor_scalar(oh, iota5, dstrel[:, ds(j, 1)], None, ALU.is_equal).then_inc(sem(f"p{ph}_edge"), 1)
            dve.wait_ge(sem(f"p{ph}_edge"), 2 * EC * (c + 1))
            Link(dve, f"dve_slow{ph}", c)(nc.vector.tensor_scalar(dstrel, dstrel, float(-C), None, ALU.add))

        def pe_slow(pe, ph, c, full, accs, w):
            n = width(full)
            for a in accs:
                nc.tensor.matmul(a, zeros[:, 0:128], zeros[:, 0:n], start=True, stop=False, skip_group_check=True)
            with pe.Fori(0, EC) as j:
                u = c * EC + j
                pe.wait_ge(sem(f"p{ph}_edge"), 2 * u + 2)
                if w:
                    pe.wait_ge(sem(f"p{ph}_gathered"), 16 * u + 16)
                for h, a in enumerate(accs):
                    for part in range(2 if w else 1):
                        lhs = gbuf[:, part * w + h * 128:part * w + h * 128 + 128] if w else onesh
                        last = nc.tensor.matmul(a, lhs, oh[:, 0:n], start=False, stop=False, skip_group_check=True)
                last.then_inc(sem(f"p{ph}_edge_used"), 1)
            for a in accs:
                last = nc.tensor.matmul(a, zeros[:, 0:128], zeros[:, 0:n], start=False, stop=True, skip_group_check=True)
            return last

        def dve_layers(dve, slow):
            if slow:
                dve.wait_ge(sem("slow_consts"), 3)
                dve.sem_inc(sem("p0_edge_used"), 1)
                Link(dve, "dve_s0")(nc.vector.tensor_copy(dstrel, dstf))

                def degrees(c, full):
                    n = width(full)
                    lk = Link(dve, "dve_s1", c)
                    dve_slow(dve, 0, c)
                    dve.wait_ge(sem("p0_agg"), c + 1)
                    wait_past(dve, "inv_out", 16 * c)
                    lk(nc.vector.tensor_scalar(invc[:, 0:n], bank(2, n), 1.0, None, ALU.max))
                    nc.vector.reciprocal(invc[:, 0:n], invc[:, 0:n]).then_inc(sem("sd_inv"), 1)
                chunks(dve, degrees)

            def slow_reset(ph):
                if slow:
                    dve.sem_inc(sem(f"p{ph}_edge_used"), 1)
                    Link(dve, f"dve_s{ph + 1}")(nc.vector.tensor_copy(dstrel, dstf))

            def group(g, slot, full, wait):
                wait_past(dve, "counted", wait)
                nw = GW if full else 1
                win = g * GW if full else NFULL * S * GW + (g - NFULL * S)
                shape = [128, 2, P, nw]
                last = nc.vector.tensor_tensor(onehots[slot][:, :, :, 0:nw], iota4[:, :, 0:nw].unsqueeze(1).to_broadcast(shape),
                                               keys[:, :, ds(win, nw)].unsqueeze(2).to_broadcast(shape), ALU.is_equal)
                last.then_inc(sem("onehot"), 1)

            def build_a(c, full):
                group(c * S, SLOT0, full, 0)

            def build_b(c, full):
                for i in (1, 2, 3):
                    group(c * S + i, i - 1, full, c * S + i - 3)

            def build_c(c, full, a, b):
                with dve.Fori(a, b) as h:
                    for k in range(3):
                        g = c * S + 3 * h + 4 + k
                        group(g, k, full, g - 2)

            def degrees_of_windows():
                lk = Link(dve, "dve_deg")
                dve.wait_ge(sem("below_sums"), 1)
                lk(nc.vector.tensor_copy(cnt, bank(7, QG * (WD + 1), P)))
                sums = cnt.rearrange("p (g j) -> p g j", j=WD + 1)
                lk(nc.vector.tensor_tensor(deg.rearrange("p (g j) -> p g j", j=WD), sums[:, :, 1:WD + 1], sums[:, :, 0:WD],
                                           ALU.subtract))
                lk(nc.vector.tensor_scalar(deg, deg, 1.0, None, ALU.max))
                nc.vector.reciprocal(deg, deg).then_inc(sem("inverse"), 1)

            def agg_out(c, full):
                n = width(full)
                dve.wait_ge(sem("p1_inv"), 16 * c + 16)
                dve.wait_ge(sem("p1_agg"), c + 1)
                wait_past(dve, "p1_h1", 2 * c)
                nc.vector.tensor_tensor(aggT[:, 0:n], bank(2, n), invc[:, 0:n], ALU.mult).then_inc(sem("p1_agg_out"), 1)

            def self_out(c, full):
                n = width(full)
                dve.wait_ge(sem("p1_selfs"), c + 1)
                wait_past(dve, "p1_self_out", 16 * c)
                nc.vector.tensor_scalar(selfT[:, 0:n], bank(7, n), b2c, None, ALU.add).then_inc(sem("p1_self"), 1)

            def low(c, full):
                nt = width(full) // P
                dve.wait_ge(sem("p1_high"), c + 1)
                nc.vector.tensor_tensor(hs_write(hbz, c, full, 1, D), tiles(bank(3, nt * D, P), D),
                                        hs_write(hbz, c, full, 0, D), ALU.subtract).then_inc(sem("p1_low"), 1)

            def slow1(c, full):
                dve_slow(dve, 1, c)
                agg_out(c, full)
                self_out(c, full)
                low(c, full)

            def step1(c, full, nxt, first=False, second=False):
                if nxt is not None:
                    build_a(c + 1, nxt)
                if not first:
                    agg_out(c - 1, True)
                if nxt is not None:
                    build_b(c + 1, nxt)
                if not first and not second:
                    low(c - 2, True)
                if nxt is not None:
                    build_c(c + 1, nxt, 0, 5)
                if not first:
                    self_out(c - 1, True)
                if nxt is not None:
                    build_c(c + 1, nxt, 5, 7)

            slow_reset(1)
            if slow:
                chunks(dve, slow1)
            else:
                build_a(0, True)
                build_b(0, True)
                degrees_of_windows()
                build_c(0, True, 0, 7)
                step1(0, True, True, first=True)
                step1(1, True, True, second=True)
                with dve.Fori(2, NFULL - 1) as c:
                    step1(c, True, True)
                step1(NFULL - 1, True, False)
                step1(NFULL, False, None)
                agg_out(NFULL, False)
                low(NFULL - 1, True)
                self_out(NFULL, False)
                low(NFULL, False)

            slow_reset(2)
            dve.wait_ge(sem("p1_self_out"), 16 * NCH)

            def step2(c, full, first=False):
                n = width(full)
                nt = n // P
                lk = Link(dve, "dve2", 3 * c)
                if slow:
                    dve_slow(dve, 2, c)
                o2 = aggT[:, 0:n]
                dve.wait_ge(sem("p2_inv"), 16 * c + 16)
                dve.wait_ge(sem("p2_agg"), c + 1)
                wait_past(dve, "p2_turned", c)
                nc.vector.scalar_tensor_tensor(o2, ps[:, ds(c * BANK, n)], izs, invc[:, 0:n], ALU.mult, ALU.mult).then_inc(
                    sem("p2_agg_out"), 1)
                dve.wait_ge(sem("p2_agg_out"), c + 1)
                dve.wait_ge(sem("p2_self"), 16 * c + 16)
                nc.vector.tensor_tensor(o2, o2, selfc[:, 0:n], ALU.add).then_inc(sem("p2_sum"), 1)
                if not first:
                    low2(c - 1, True)
                bc = lambda a: a.unsqueeze(2).to_broadcast([P, nt, D])
                v = lambda t: tiles(t[:, 0:nt * D], D)
                m, sm, ls = st[0:P, 0:nt], st[0:P, 4:4 + nt], st[0:P, 8:8 + nt]
                y = tiles(bank(7, nt * D, P), D)
                dve.wait_ge(sem("p2_turned"), c + 1)
                lk(nc.vector.tensor_reduce(m, y, AX, ALU.max))
                nc.vector.tensor_tensor(v(yc), y, bc(m), ALU.subtract).then_inc(sem("p2_shifted"), 1)
                dve.wait_ge(sem("p2_shifted"), c + 1)
                dve.wait_ge(sem("p2_x"), 16 * c + 16)
                wait_past(dve, "p2_x1_out", 16 * c)
                nc.vector.tensor_tensor(v(x1b), v(xin), v(yc), ALU.add).then_inc(sem("p2_x_used"), 1)
                dve.wait_ge(sem("p2_exp"), c + 1)
                nc.vector.tensor_reduce(sm, v(sqb), AX, ALU.add).then_inc(sem("p2_expsum"), 1)
                dve.wait_ge(sem("p2_lse"), c + 1)
                dve.wait_ge(sem("p2_x_used"), c + 1)
                nc.vector.tensor_tensor(v(x1b), v(x1b), bc(ls), ALU.subtract).then_inc(sem("p2_x1"), 1)
                dve.wait_ge(sem("p2_x1"), c + 1)
                dve.sem_inc(sem("p2_x1_seen"), 1)
                ln_stats(lk, x1b, yc, nt, bns, mv, st[0:P, 12:12 + nt], "p2_", in_loop=True)

            def low2(c, full):
                dve.wait_ge(sem("p2_high"), c + 1)
                nc.vector.tensor_tensor(hs_write(ha, c, full, 1, D), tiles(sqb[:, 0:width(full) // P * D], D),
                                        hs_write(ha, c, full, 0, D), ALU.subtract).then_inc(sem("p2_low"), 1)
            step2(0, True, True)
            step2(1, True)
            with dve.Fori(2, NFULL) as c:
                step2(c, True)
            step2(NFULL, False)
            low2(NFULL, False)

            slow_reset(3)
            dve.wait_ge(sem("p2_x1_out"), 16 * NCH)

            def low3(c, full):
                for k, (t0, t1) in enumerate(HALVES[full]):
                    dve.wait_ge(sem("p3_high"), 2 * c + k + 1)
                    nc.vector.tensor_tensor(hs_write(hbz, c, full, 1, H)[:, t0:t1], tiles(bank(6 + k, (t1 - t0) * H, P), H),
                                            hs_write(hbz, c, full, 0, H)[:, t0:t1], ALU.subtract).then_inc(sem("p3_low"), 1)

            def step3(c, full, first=False):
                n = width(full)
                if slow:
                    dve_slow(dve, 3, c)
                dve.wait_ge(sem("p3_inv"), 16 * c + 16)
                dve.wait_ge(sem("p3_agg"), c + 1)
                wait_past(dve, "p3_h3", 2 * c)
                nc.vector.tensor_tensor(aggT[:, 0:n], bank(acc3(c, slow), n), invc[:, 0:n], ALU.mult).then_inc(
                    sem("p3_agg_out"), 1)
                if not first:
                    low3(c - 1, True)
            step3(0, True, first=True)
            step3(1, True)
            with dve.Fori(2, NFULL) as c:
                step3(c, True)
            step3(NFULL, False)
            low3(NFULL, False)

            slow_reset(4)

            def step4(c, full):
                n = width(full)
                nt = n // P
                if slow:
                    dve_slow(dve, 4, c)
                dve.wait_ge(sem("p4_inv"), 16 * c + 16)
                wait_past(dve, "p4_lin2", c)
                for h in range(2):
                    dve.wait_ge(sem("p4_agg"), 2 * c + h + 1)
                    nc.vector.tensor_tensor(aggT[:, h * C:h * C + n], bank(h, n), invc[:, 0:n], ALU.mult).then_inc(
                        sem("p4_agg_out"), 1)
                dve.wait_ge(sem("p4_turned"), c + 1)
                dve.wait_ge(sem("p4_x1"), 16 * c + 16)
                wait_past(dve, "p4_out", 16 * c)
                nc.vector.tensor_tensor(outb[:, 0:nt * D], bank(3, nt * D, P), x1in[:, 0:nt * D], ALU.add).then_inc(
                    sem("p4_sum"), 1)
            chunks(dve, step4)

        def act_layers(act, slow):
            def build(c, full, a, b):
                nd = C // S if full else WD

                def group(g, k):
                    act.wait_ge(sem("counted"), g + 1)
                    at = g * (C // S) if full else NFULL * C + (g - NFULL * S) * WD
                    v = adj[0:P, 0:S * N].rearrange("p (t n) -> p t n", n=N)
                    nc.scalar.activation(v[:, :, ds(at, nd)], bank(k, nd * S, P).rearrange("p (d t) -> p t d", t=S),
                                         ACT.Copy).then_inc(sem("evicted"), 1)
                if a == 0:
                    group(c * S, SLOT0 if b == 0 else 0)
                if b == 0:
                    with act.Fori(0, (S - 1) // 3) as h:
                        for k in range(3):
                            group(3 * h + 1 + k, k)
                    return
                with act.Fori(a // 2, b // 2) as h:
                    group(c * S + 1 + 2 * h, 1)
                    group(c * S + 2 + 2 * h, 0)

            def h0_turned(c, full):
                n = width(full)
                act.wait_ge(sem("p1_own"), c + 1)
                wait_past(act, "p1_h1", 2 * c)
                nc.scalar.activation(aggT[:, C:C + n], bank(6, n), ACT.Copy).then_inc(sem("p1_h0T"), 1)

            def relu(c, full):
                n = width(full)
                wait_past(act, "p1_selfs", c)
                for m in range(2):
                    act.wait_ge(sem("p1_h1"), 2 * c + m + 1)
                    nc.scalar.activation(actT[:, m * C:m * C + n], bank(4 + m, n), ACT.Relu, bias=b1c[:, m:m + 1]).then_inc(
                        sem("p1_relu"), 1)

            def z_out(c, full):
                n = width(full)
                act.wait_ge(sem("p1_zm"), c + 1)
                wait_past(act, "p1_turned", c)
                nc.scalar.activation(zT[:, 0:n], bank(6, n), ACT.Identity, scale=zs).then_inc(sem("p1_zT"), 1)

            def high(c, full):
                nt = width(full) // P
                act.wait_ge(sem("p1_turned"), c + 1)
                nc.scalar.activation(hs_write(hbz, c, full, 0, D), tiles(bank(3, nt * D, P), D), ACT.Copy).then_inc(
                    sem("p1_high"), 1)

            def whole(c, full):
                for part in (h0_turned, relu, z_out, high):
                    part(c, full)

            def step1(c, full, nxt, first=False, second=False):
                if not first:
                    h0_turned(c - 1, True)
                    if not second:
                        high(c - 2, True)
                for part, a, b in ((relu, 0, CUT1), (z_out, CUT1, CUT2), (None, CUT2, S - 1)):
                    if nxt is not None:
                        build(c + 1, nxt, a, b)
                    if part and not first:
                        part(c - 1, True)

            if slow:
                chunks(act, whole)
            else:
                act.wait_ge(sem("wt_out"), 16)
                act.wait_ge(sem("onehot"), 1)
                build(0, True, 0, 0)
                step1(0, True, True, first=True)
                act.wait_ge(sem("inv_out"), 16)
                step1(1, True, True, second=True)
                with act.Fori(2, NFULL - 1) as c:
                    step1(c, True, True)
                step1(NFULL - 1, True, False)
                step1(NFULL, False, None)
                high(NFULL - 1, True)
                whole(NFULL, False)

            def step2(c, full):
                nt = width(full) // P
                v = lambda t: t[:, 0:nt * D]
                act.wait_ge(sem("p2_shifted"), c + 1)
                nc.scalar.activation(v(sqb), v(yc), ACT.Exp).then_inc(sem("p2_exp"), 1)
                act.wait_ge(sem("p2_expsum"), c + 1)
                nc.scalar.activation(st[0:P, 8:8 + nt], st[0:P, 4:4 + nt], ACT.Ln).then_inc(sem("p2_lse"), 1)
                act.wait_ge(sem("p2_centred"), c + 1)
                act.wait_ge(sem("p2_rstd"), c + 1)
                for t in range(nt):
                    last = nc.scalar.activation(sqb[:, t * D:(t + 1) * D], yc[:, t * D:(t + 1) * D], ACT.Relu,
                                                scale=st[0:P, 16 + t:17 + t])
                last.then_inc(sem("p2_relu"), 1)
                act.wait_ge(sem("p2_relu"), c + 1)
                nc.scalar.activation(hs_write(ha, c, full, 0, D), tiles(v(sqb), D), ACT.Copy).then_inc(sem("p2_high"), 1)
            chunks(act, step2)

            act.wait_ge(sem("p2_x1_out"), 16 * NCH)

            def step3(c, full):
                n = width(full)
                nt = n // P
                act.wait_ge(sem("p3_own"), c + 1)
                wait_past(act, "p3_h3", 2 * c)
                nc.scalar.activation(aggT[:, C:C + n], bank(3, n), ACT.Copy).then_inc(sem("p3_ownT"), 1)
                wait_past(act, "p3_turned", 2 * c)
                for m in range(2):
                    act.wait_ge(sem("p3_h3"), 2 * c + m + 1)
                    nc.scalar.activation(actT[:, m * C:m * C + n], bank(4 + m, n), ACT.Relu, bias=b3s[:, m:m + 1],
                                         scale=s3[:, m:m + 1]).then_inc(sem("p3_relu"), 1)
                for k, (t0, t1) in enumerate(HALVES[full]):
                    act.wait_ge(sem("p3_turned"), 2 * c + k + 1)
                    nc.scalar.activation(hs_write(hbz, c, full, 0, H)[:, t0:t1], tiles(bank(6 + k, (t1 - t0) * H, P), H),
                                         ACT.Copy).then_inc(sem("p3_high"), 1)
            chunks(act, step3)

            h3T = wts[:, 0:2 * C]

            def step4(c, full):
                n = width(full)
                for m in range(2):
                    act.wait_ge(sem("p4_own"), 2 * c + m + 1)
                    if m == 0:
                        wait_past(act, "p4_turned", c)
                    nc.scalar.activation(h3T[:, m * C:m * C + n], bank(2 + m, n), ACT.Copy).then_inc(sem("p4_ownT"), 1)
                for m in range(2):
                    act.wait_ge(sem("p4_h4"), 2 * c + m + 1)
                    nc.scalar.activation(actT[:, m * C:m * C + n], bank(4 + m, n), ACT.Relu, bias=bl1c[:, m:m + 1]).then_inc(
                        sem("p4_relu"), 1)
                for m in range(2):
                    act.wait_ge(sem("p4_lin1"), 2 * c + m + 1)
                    nc.scalar.activation(aggT[:, m * C:m * C + n], bank(6 + m, n), ACT.Relu, bias=bac[:, m:m + 1]).then_inc(
                        sem("p4_relu2"), 1)
                act.wait_ge(sem("p4_lin2"), c + 1)
                nc.scalar.activation(h3T[:, 0:n], bank(2, n), ACT.Identity, bias=bbc).then_inc(sem("p4_lin2T"), 1)
            chunks(act, step4)

        def pe_layers(pe, slow):
            def aggregate(acc, hs, w, h, c, full, s):
                n = width(full)
                for part in range(2):
                    last = nc.tensor.matmul(acc[:, 0:n], hs[:, ds(s * (2 * w) + part * w + h * 128, 128)],
                                            adj[0:P, ds(s * N + c * C, n)],
                                            start=(isinstance(s, int) and s == 0 and part == 0),
                                            stop=(isinstance(s, int) and s == S - 1 and part == 1), skip_group_check=True)
                return last

            def own(hs, w, h, b, c, full):
                for t in range(width(full) // P):
                    for part in range(2):
                        last = nc.tensor.matmul(bank(b)[:, t * P:(t + 1) * P],
                                                hs[:, ds((c * 4 + t) * (2 * w) + part * w + h * 128, 128)],
                                                identh[0:P, 0:P], start=(part == 0), stop=(part == 1))
                return last

            def dense(b, n, terms):
                for k, (wt, v) in enumerate(terms):
                    last = nc.tensor.matmul(bank(b, n), wt, v, start=(k == 0), stop=(k == len(terms) - 1))
                return last

            if slow:
                pe.wait_ge(sem("slow_consts"), 3)

                def degrees(c, full):
                    wait_past(pe, "sd_inv", c)
                    pe_slow(pe, 0, c, full, [bank(2, width(full))], 0).then_inc(sem("p0_agg"), 1)
                chunks(pe, degrees)

            def count(g, i, c_full, wait, b=None):
                pe.wait_ge(sem("onehot"), g + 1)
                wait_past(pe, "evicted", wait)
                slot = (i - 1) % 3 if i else SLOT0
                for w in range(GW if c_full else 1):
                    last = nc.tensor.matmul(bank(i % 2 if b is None else b)[0:P, w * WD * S:(w + 1) * WD * S], onehots[slot][:, 0, :, w],
                                            onehots[slot][:, 1, :, w], start=True, stop=True)
                last.then_inc(sem("counted"), 1)

            def own1(c, full):
                wait_past(pe, "p1_zT", c)
                own(ha, D, 0, 6, c, full).then_inc(sem("p1_own"), 1)

            def hidden1(c, full):
                n = width(full)
                wait_past(pe, "p1_relu", 2 * c)
                pe.wait_ge(sem("p1_h0T"), c + 1)
                pe.wait_ge(sem("p1_agg_out"), c + 1)
                for m in range(2):
                    dense(4 + m, n, [(w1v[:, 0, m * 128:m * 128 + 128], aggT[:, C:C + n]),
                                     (w1v[:, 1, m * 128:m * 128 + 128], aggT[:, 0:n])]).then_inc(sem("p1_h1"), 1)

            def second1(c, full):
                n = width(full)
                pe.wait_ge(sem("p1_relu"), 2 * c + 2)
                dense(6, n, [(w2v[:, 2 + m, :], actT[:, m * C:m * C + n]) for m in range(2)]).then_inc(sem("p1_zm"), 1)
                wait_past(pe, "p1_self", c)
                dense(7, n, [(w2v[:, m, :], actT[:, m * C:m * C + n]) for m in range(2)]).then_inc(sem("p1_selfs"), 1)

            def turn1(c, full):
                pe.wait_ge(sem("p1_zT"), c + 1)
                wait_past(pe, "p1_low", c)
                for t in range(width(full) // P):
                    last = nc.tensor.transpose(bank(3, 4 * D, P)[:, t * D:(t + 1) * D], zT[:, t * P:(t + 1) * P], identf[:])
                last.then_inc(sem("p1_turned"), 1)

            def slow1(c, full):
                wait_past(pe, "p1_agg_out", c)
                pe_slow(pe, 1, c, full, [bank(2, width(full))], D).then_inc(sem("p1_agg"), 1)
                for part in (own1, hidden1, second1, turn1):
                    part(c, full)

            def step1(c, full, nxt, first=False):
                acc = bank(2)
                g = (c + 1) * S

                def pieces(a, b, at=0):
                    for i in range(a, b):
                        if nxt is not None:
                            count(g + at + i, i, nxt, g + at + i - 1)
                        last = aggregate(acc, ha, D, 0, c, full, at + i)
                    return last

                def looped(a, b):
                    with pe.Fori(a // 6, b // 6) as h:
                        pieces(1, 7, 6 * h)
                if not first:
                    own1(c - 1, True)
                if nxt is not None:
                    count(g, 0, nxt, g)
                pe.wait_ge(sem("evicted"), g)
                wait_past(pe, "p1_agg_out", c)
                aggregate(acc, ha, D, 0, c, full, 0)
                looped(0, CUT1)
                if not first:
                    hidden1(c - 1, True)
                looped(CUT1, CUT2)
                if not first:
                    second1(c - 1, True)
                looped(CUT2, S - 7)
                pieces(S - 6, S).then_inc(sem("p1_agg"), 1)
                if not first:
                    turn1(c - 1, True)

            if slow:
                pe.wait_ge(sem("n_low"), 1)
                pe.wait_ge(sem("w1_scaled"), 1)
                pe.wait_ge(sem("p1_rows"), 16)
                chunks(pe, slow1)
            else:
                count(0, 0, True, 0, b=SLOT0)
                for i in (1, 2, 3):
                    count(i, i, True, 0, b=i - 1)
                with pe.Fori(1, (S - 1) // 3) as h:
                    for k in range(3):
                        count(3 * h + 1 + k, 1 + k, True, 3 * h + k - 1, b=k)
                pe.wait_ge(sem("n_low"), 1)
                pe.wait_ge(sem("w1_scaled"), 1)
                step1(0, True, True, first=True)
                step1(1, True, True)
                with pe.Fori(2, NFULL - 1) as c:
                    step1(c, True, True)
                step1(NFULL - 1, True, False)
                step1(NFULL, False, None)

            def staged(ph, aggs, parts, lead, source, fill=(0, 0)):
                def slow_step(c, full):
                    if ph > 2:
                        wait_past(pe, f"p{ph}_agg_out", len(aggs) * c)
                    pe_slow(pe, ph, c, full, [a[0](c)[:, 0:width(full)] for a in aggs], aggs[0][2]).then_inc(
                        sem(f"p{ph}_agg"), len(aggs))
                    for _, p, _ in parts:
                        p(c, full)
                if slow:
                    pe.wait_ge(sem(f"p{ph - 1}_low"), source[2])
                    pe.wait_ge(sem(f"p{ph}_rows"), 16)
                    chunks(pe, slow_step)
                    return
                pe.wait_ge(sem(f"p{ph - 1}_low"), source[0])

                def tile(c, full, at):
                    acc, hs, w, h = aggs[at // S]
                    last = aggregate(acc(c), hs, w, h, c, full, at % S)
                    if at % S == S - 1:
                        last.then_inc(sem(f"p{ph}_agg"), 1)

                def step0():
                    ahead = 0
                    for at in range(len(aggs) * S):
                        for tiles_done, part, of in lead:
                            if at == tiles_done:
                                part(of, of < NFULL)
                        for k, first_late in enumerate(((NFULL - 1) * (C // P), S - 1)):
                            if at == first_late:
                                for _ in range(fill[k]):
                                    tile(1, True, ahead)
                                    ahead += 1
                                pe.wait_ge(sem(f"p{ph - 1}_low"), source[1 + k])
                        tile(0, True, at)

                def step(c, full):
                    done = sum(fill) if isinstance(c, int) and c == 1 else 0
                    for at in range(len(aggs) * S):
                        for tiles_done, part, lag in parts:
                            if at == (tiles_done and tiles_done + done) and (not isinstance(c, int) or c >= lag):
                                part(c - lag, True)
                        if at == 0 and ph > 2 and not done:
                            wait_past(pe, f"p{ph}_agg_out", len(aggs) * c)
                        if at >= done:
                            tile(c, full, at)
                step0()
                step(1, True)
                with pe.Fori(2, NFULL) as c:
                    step(c, True)
                step(NFULL, False)

            each_own = lambda c: ps[:, ds(c * BANK, BANK)]
            fixed = lambda b: lambda c: bank(b)

            def turn2(c, full):
                pe.wait_ge(sem("p2_sum"), c + 1)
                wait_past(pe, "p2_shifted", c)
                for t in range(width(full) // P):
                    last = nc.tensor.transpose(bank(7, 4 * D, P)[:, t * D:(t + 1) * D], aggT[:, t * P:(t + 1) * P], identf[:])
                last.then_inc(sem("p2_turned"), 1)
            staged(2, [(each_own, hbz, D, 0)], [(7, turn2, 1)],
                   [(0, own1, NFULL), (6, hidden1, NFULL), (12, second1, NFULL), (17, turn1, NFULL)], (NFULL - 1, NFULL, NCH))

            pe.wait_ge(sem("w0_in"), 16)

            def own3(c, full):
                wait_past(pe, "p3_ownT", c)
                own(ha, D, 0, 3, c, full).then_inc(sem("p3_own"), 1)

            def hidden3(c, full):
                n = width(full)
                pe.wait_ge(sem("p3_ownT"), c + 1)
                pe.wait_ge(sem("p3_agg_out"), c + 1)
                wait_past(pe, "p3_relu", 2 * c)
                for m in range(2):
                    dense(4 + m, n, [(wts[:, 256 + m * 128:384 + m * 128], aggT[:, C:C + n]),
                                     (wts[:, m * 128:m * 128 + 128], aggT[:, 0:n])]).then_inc(sem("p3_h3"), 1)

            def turn3(c, full):
                pe.wait_ge(sem("p3_relu"), 2 * c + 2)
                wait_past(pe, "p3_low", 2 * c)
                for k, (t0, t1) in enumerate(HALVES[full]):
                    for t in range(t0, t1):
                        for m in range(2):
                            at = ((t - t0) * 2 + m) * 128
                            last = nc.tensor.transpose(bank(6 + k, 4 * D, P)[:, at:at + 128],
                                                       actT[:, m * C + t * P:m * C + (t + 1) * P], identf[:])
                    last.then_inc(sem("p3_turned"), 1)
            staged(3, [(lambda c: bank(acc3(c, slow)), ha, D, 0)], [(0, own3, 1), (8, hidden3, 1), (0, turn3, 2)],
                   [(14, turn2, NFULL)], (NFULL - 1, NFULL, NCH), fill=(5, 8))

            l1v = w4[:, 0:512].rearrange("p (k o) -> p k o", k=2)
            r1v = w4[:, 512:1024].rearrange("p (k o) -> p k o", k=2)
            av = w4[:, 1024:1536].rearrange("p (k o) -> p k o", k=2)
            bv = w4[:, 1536:1792].rearrange("p (k o) -> p k o", k=2)
            h3T = wts[:, 0:2 * C]

            def own4(c, full):
                wait_past(pe, "p4_lin2T", c)
                own(hbz, H, 0, 2, c, full).then_inc(sem("p4_own"), 1)
                wait_past(pe, "p4_sum", c)
                own(hbz, H, 1, 3, c, full).then_inc(sem("p4_own"), 1)

            def hidden4(c, full):
                n = width(full)
                pe.wait_ge(sem("w4_in"), 16)
                pe.wait_ge(sem("p4_ownT"), 2 * c + 2)
                pe.wait_ge(sem("p4_agg_out"), 2 * c + 2)
                wait_past(pe, "p4_relu", 2 * c)
                for m in range(2):
                    o = slice(m * 128, m * 128 + 128)
                    dense(4 + m, n, [(r1v[:, 0, o], h3T[:, 0:n]), (r1v[:, 1, o], h3T[:, C:C + n]),
                                     (l1v[:, 0, o], aggT[:, 0:n]), (l1v[:, 1, o], aggT[:, C:C + n])]).then_inc(sem("p4_h4"), 1)

            def lin1(c, full):
                n = width(full)
                pe.wait_ge(sem("p4_relu"), 2 * c + 2)
                wait_past(pe, "p4_relu2", 2 * c)
                for m in range(2):
                    o = slice(m * 128, m * 128 + 128)
                    dense(6 + m, n, [(av[:, k, o], actT[:, k * C:k * C + n]) for k in range(2)]).then_inc(sem("p4_lin1"), 1)

            def lin2(c, full):
                n = width(full)
                pe.wait_ge(sem("p4_relu2"), 2 * c + 2)
                dense(2, n, [(bv[:, k, :], aggT[:, k * C:k * C + n]) for k in range(2)]).then_inc(sem("p4_lin2"), 1)

            def turn4(c, full):
                pe.wait_ge(sem("p4_lin2T"), c + 1)
                for t in range(width(full) // P):
                    last = nc.tensor.transpose(bank(3, 4 * D, P)[:, t * D:(t + 1) * D], h3T[:, t * P:(t + 1) * P], identf[:])
                last.then_inc(sem("p4_turned"), 1)
            staged(4, [(fixed(0), hbz, H, 0), (fixed(1), hbz, H, 1)],
                   [(0, own4, 1), (10, hidden4, 1), (20, lin1, 1), (30, lin2, 1), (40, turn4, 1)],
                   [(0, own3, NFULL), (0, turn3, NFULL - 1), (8, hidden3, NFULL), (16, turn3, NFULL)],
                   (2 * NFULL - 2, 2 * NFULL, 2 * NCH - 1))
            if not slow:
                for part in (own4, hidden4, lin1, lin2, turn4):
                    part(NFULL, False)

        @block.sync
        def _(sp):
            sp.dma_start(dst_i, dst.rearrange("(r e) -> r e", r=ER)).then_inc(sem("dst_in"), 16)
            sp.dma_start(src_i, src.rearrange("(r e) -> r e", r=ER)).then_inc(sem("src_in"), 16)
            sp.wait_ge(sem("padk"), 1)
            sp.dma_start(key_d[E:E + 250].rearrange("(o e) -> o e", o=1), padk[0:1, 0:250]).then_inc(sem("key_out"), 16)

            def load_x(t0, t1, name):
                sp.dma_start(tiles(xs0[:, t0 * D:t1 * D], D),
                             x[t0 * P:t1 * P, :].rearrange("(t p) d -> p t d", p=P)).then_inc(sem(name), 16)

            def load_w(name, w):
                at, kt, mt = WN[name]
                sp.dma_start(wn[:, at:at + kt * mt * 128].rearrange("p (m k) -> p m k", m=mt),
                             w.rearrange("(m p) k -> p m k", p=128)).then_inc(sem("w_in"), 16)
            natural = (("l0", Wl0), ("r0", Wr0), ("l1", Wl1), ("r1", Wr1), ("a", Wa), ("b", Wb))
            load_x(0, XA, "x_in_a")
            for name, w in natural[0:3]:
                load_w(name, w)
            sp.wait_ge(sem("keys"), 1)
            sp.dma_start(key_d[0:E].rearrange("(r e) -> r e", r=ER), keyf).then_inc(sem("key_out"), 16)
            load_x(XA, S, "x_in_b")
            for name, w in natural[3:]:
                load_w(name, w)
            sp.dma_start(w1v, W1.rearrange("(k p) o -> p k o", p=128)).then_inc(sem("w_in"), 16)
            sp.dma_start(w2v, W2.rearrange("(k p) o -> p k o", p=128)).then_inc(sem("w_in"), 16)
            for dstc, b, k in ((b1c, b1, 2), (bl0c, bl0, 2), (bl1c, bl1, 2), (bac, ba, 2), (b2c, b2, 1), (bbc, bb, 1)):
                with nc.allow_non_contiguous_dma(reason="one bias per partition"):
                    sp.dma_start(dstc, b.rearrange("(k p) -> p k", k=k)).then_inc(sem("w_in"), 16)
            sp.wait_ge(sem("wt"), 5)
            sp.wait_ge(sem("relative"), QG)
            sp.dma_start(wt_d, wt_s).then_inc(sem("wt_out"), 16)
            branch(sp, sp_layers)

        @block.gpsimd
        def _(pool):
            nc.gpsimd.memset(identf[:], 0.0).then_inc(sem("pool"), 1)
            nc.gpsimd.memset(identh[:], 0.0).then_inc(sem("pool"), 1)
            nc.gpsimd.memset(padk[:, :], 1.2e7).then_inc(sem("padk"), 1)
            nc.gpsimd.memset(onesf[:, :], 1.0).then_inc(sem("ones"), 1)
            nc.gpsimd.memset(ones_c, 1.0).then_inc(sem("ones"), 1)
            nc.gpsimd.memset(ones_h, 1.0).then_inc(sem("ones"), 1)
            nc.gpsimd.memset(mhalf0, -0.5).then_inc(sem("mhalf0"), 1)
            nc.gpsimd.memset(mhalf, -0.5).then_inc(sem("mhalf"), 1)
            pool.wait_ge(sem("pool"), 2)
            for t in (identf, identh):
                nc.gpsimd.affine_select(out=t[:], in_=t[:], compare_op=ALU.not_equal, fill=1.0, base=0,
                                        pattern=[[-1, 128]], channel_multiplier=1).then_inc(sem("ident"), 1)
            nc.gpsimd.iota(thr, [[WD * P, QG]], base=0, channel_multiplier=WD,
                           allow_small_or_imprecise_dtypes=True).then_inc(sem("iota"), 1)
            nc.gpsimd.iota(iota4, [[1, P], [0, GW]], base=0, channel_multiplier=0,
                           allow_small_or_imprecise_dtypes=True).then_inc(sem("iota"), 1)
            pool.wait_ge(sem("rowi"), 1)
            pool.wait_ge(sem("key_out"), 32)
            for g in range(QG):
                pool.indirect_dma_start(rows[:, g * EC:(g + 1) * EC], None,
                                        key_d[0:E].rearrange("(r e) -> r e", e=EC),
                                        bass.IndirectOffsetOnAxis(rowi[:, g:g + 1], 0)).then_inc(sem(f"gathered{g}"), 16)
            pool.wait_ge(sem("mhalf0"), 1)
            pool.wait_ge(sem("n_var"), 2)
            nc.gpsimd.tensor_tensor(rstd0, var0, mhalf0, ALU.pow).then_inc(sem("n_rstd"), 1)
            pool.wait_ge(sem("n_rstd"), 1)
            nc.gpsimd.tensor_tensor(nmr0, nmean0, rstd0, ALU.mult).then_inc(sem("n_rstd"), 1)
            pool.wait_ge(sem("starti"), 1)
            for g in range(QG):
                pool.indirect_dma_start(gk[:, g * CAP:(g + 1) * CAP], None,
                                        key_d.rearrange("(e o) -> e o", o=1),
                                        bass.IndirectOffsetOnAxis(starti[:, g:g + 1], 0)).then_inc(sem(f"gathered{g}"), 16)
            pool.wait_ge(sem("n_high"), 1)
            nc.gpsimd.tensor_tensor(h0v[:, :, 1, :], tiles(xs0, D), h0v[:, :, 0, :], ALU.subtract).then_inc(sem("n_low"), 1)
            branch(pool, pool_layers)

        @block.vector
        def _(dve):
            lk = Link(dve, "dve")
            dve.wait_ge(sem("dst_in"), 16)
            nc.vector.tensor_copy(dstf, dst_i).then_inc(sem("dstf"), 1)
            dve.wait_ge(sem("src_in"), 16)
            lk(nc.vector.tensor_scalar(t_i, src_i, float(DIV_M), None, ALU.mult))
            lk(nc.vector.tensor_scalar(s_i, t_i, DIV_S, None, ALU.logical_shift_right))
            dve.wait_ge(sem("dstf"), 1)
            lk(nc.vector.scalar_tensor_tensor(keyf, dstf, float(S * KEY), src_i, ALU.mult, ALU.add))
            nc.vector.scalar_tensor_tensor(keyf, s_i, float(KEY - P), keyf, ALU.mult, ALU.add).then_inc(sem("keys"), 1)
            dve.wait_ge(sem("ident"), 2)
            nc.vector.tensor_scalar(diag, identf[0:ER, 0:ER], dstf[:, 0:1], None, ALU.mult).then_inc(sem("diag"), 1)
            dve.wait_ge(sem("iota"), 2)
            dve.wait_ge(sem("firsts"), 1)
            for g in range(QG):
                last = nc.vector.tensor_scalar(junk[g][:, 0:ER], bank(0, ER, P), thr[:, g:g + 1], None, ALU.is_lt, ALU.add,
                                               accum_out=rowf[:, g:g + 1])
            lk(last)
            lk(nc.vector.tensor_scalar(rowf, rowf, -1.0, 0.0, ALU.add, ALU.max))
            nc.vector.tensor_copy(rowi, rowf).then_inc(sem("rowi"), 1)
            nc.vector.tensor_scalar(wbase, thr, float(S * KEY), None, ALU.mult).then_inc(sem("wbase"), 1)
            for t in range(S):
                if t in (0, XA):
                    dve.wait_ge(sem("x_in_b" if t else "x_in_a"), 16)
                last = nc.vector.bn_stats(bns0[:, 6 * t:6 * t + 6], xs0[:, t * D:(t + 1) * D])
            last.then_inc(sem("n_stats"), 1)
            dve.wait_ge(sem("n_stats"), 1)
            for t in range(S):
                last = nc.vector.bn_aggr(mv0[:, 2 * t:2 * t + 2], bns0[:, 6 * t:6 * t + 6])
            lk(last)
            mv2 = tiles(mv0, 2)
            nc.vector.tensor_scalar(var0, mv2[:, :, 1], 1e-5, LN_SCALE ** -2, ALU.add, ALU.mult).then_inc(sem("n_var"), 1)
            nc.vector.tensor_scalar(nmean0, mv2[:, :, 0], -1.0, None, ALU.mult).then_inc(sem("n_var"), 1)
            dve.wait_ge(sem("wbase"), 1)
            for g in range(QG):
                dve.wait_ge(sem(f"gathered{g}"), 16)
                last = nc.vector.tensor_scalar(rows[:, g * EC:(g + 1) * EC], rows[:, g * EC:(g + 1) * EC], wbase[:, g:g + 1], None,
                                               ALU.is_lt, ALU.add, accum_out=inrow[:, g:g + 1])
            lk(last)
            lk(nc.vector.scalar_tensor_tensor(rowf, rowf, float(EC), inrow, ALU.mult, ALU.add))
            nc.vector.tensor_copy(starti, rowf).then_inc(sem("starti"), 1)
            dve.wait_ge(sem("absw"), 1)
            nc.vector.tensor_reduce(bnd, wn[:, 0:256].rearrange("p (m k) -> p m k", m=2), AX, ALU.add, apply_absolute_value=True)
            lk(nc.vector.tensor_reduce(tmp2, wn[:, 256:512].rearrange("p (m k) -> p m k", m=2), AX, ALU.add,
                                       apply_absolute_value=True))
            lk(nc.vector.tensor_tensor(bnd, bnd, tmp2, ALU.add))
            lk(nc.vector.scalar_tensor_tensor(bnd, bnd, LN_BOUND, bl0a, ALU.mult, ALU.add))

            def pow2(scale, inverse, bound):
                lk(nc.vector.tensor_scalar(bound, bound, 1e-20, None, ALU.max))
                lk(nc.vector.reciprocal(bound, bound))
                lk(nc.vector.tensor_scalar(bound, bound, TOP, None, ALU.mult))
                lk(nc.vector.tensor_scalar(scale.bitcast(I32), bound.bitcast(I32), EXP_MASK, None, ALU.bitwise_and))
                lk(nc.vector.tensor_scalar(inverse.bitcast(I32), scale.bitcast(I32), -1.0, float(EXP_FLIP), ALU.mult, ALU.add))
            pow2(s3, is3, bnd)
            nc.vector.tensor_tensor(b3s, bl0c, s3, ALU.mult).then_inc(sem("scale3"), 1)
            dve.wait_ge(sem("bound1"), 1)
            nc.vector.scalar_tensor_tensor(bnd, bank(0, 2), LN_BOUND, b1a, ALU.mult, ALU.add).then_inc(sem("bound1s"), 1)
            dve.wait_ge(sem("boundz"), 1)
            lk(nc.vector.tensor_copy(bndz, bank(0, 3)[:, 2:3]))
            pow2(zs, izs, bndz)
            for g in range(QG):
                dve.wait_ge(sem(f"gathered{g}"), 32)
                v = gk[:, g * CAP:(g + 1) * CAP]
                nc.vector.tensor_scalar(v, v, wbase[:, g:g + 1], None, ALU.subtract).then_inc(sem("relative"), 1)
            dve.wait_ge(sem("keysT"), 1)
            nc.vector.tensor_copy(k_i[:, 0:4 * P], bank(2, 4 * P))
            lk(nc.vector.tensor_copy(k_i[:, 4 * P:NWIN], bank(3, P)))
            lk(nc.vector.tensor_scalar(kn_i, k_i, 7, None, ALU.arith_shift_right))
            lk(nc.vector.tensor_scalar(kn[:, :], kn_i, 200.0, -1.0, ALU.min, ALU.max))

            def lie_below(j, **sums):
                return nc.vector.tensor_scalar(below[j], kn[:, :], float(j * S), None, ALU.is_lt, **sums)
            lie_below(0, op1=ALU.add, accum_out=held[:, 0:1])
            lk(lie_below(WD, op1=ALU.add, accum_out=held[:, 1:2]))
            nc.vector.tensor_tensor(flag_f, held[:, 1:2], held[:, 0:1], ALU.subtract).then_inc(sem("held"), 1)
            for j in range(1, WD):
                last = lie_below(j)
            last.then_inc(sem("below"), 1)
            lk(nc.vector.tensor_scalar(kp_i, k_i, KEY - 1, None, ALU.bitwise_and))
            nc.vector.tensor_copy(kp[:, :], kp_i).then_inc(sem("split"), 1)
            dve.wait_ge(sem("held_sum"), 1)
            nc.vector.tensor_scalar(flag_i[0:1], bank(1, 1, 1), float(E), None, ALU.is_equal).then_inc(sem("flag"), 1)
            dve.wait_ge(sem("split"), 1)
            branch(dve, dve_layers)

        @block.scalar
        def _(act):
            act.wait_ge(sem("w_in"), 16 * NW)
            nc.scalar.activation(absw[:, 0:512], wts[:, 0:512], ACT.Abs)
            nc.scalar.activation(absw[:, 512:768], wts[:, 768:1024], ACT.Abs)
            nc.scalar.activation(b1a, b1c, ACT.Abs)
            nc.scalar.activation(bl0a, bl0c, ACT.Abs).then_inc(sem("absw"), 1)
            nc.scalar.activation(wts[:, 0:512], wts[:, 0:512], ACT.Copy, scale=1.0 / LN_SCALE).then_inc(sem("w1_scaled"), 1)
            for k in range(5):
                act.wait_ge(sem("wturned"), k + 1)
                turned = ps[:, (4 + k % 4) * BANK:(5 + k % 4) * BANK]
                if k == 0:
                    nc.scalar.activation(wt_s[:, 0:512], turned, ACT.Copy, scale=1.0 / LN_SCALE).then_inc(sem("wt"), 1)
                    act.wait_ge(sem("scale3"), 1)
                elif k < 3:
                    for kt in range(2):
                        last = nc.scalar.activation(wt_s[:, 512 * k + 256 * kt:512 * k + 256 * kt + 256],
                                                    turned[:, 256 * kt:256 * kt + 256], ACT.Identity, scale=is3[:, kt:kt + 1])
                    last.then_inc(sem("wt"), 1)
                else:
                    n = 512 if k == 3 else 256
                    nc.scalar.activation(wt_s[:, 512 * k:512 * k + n], turned[:, 0:n], ACT.Copy).then_inc(sem("wt"), 1)
            act.wait_ge(sem("n_rstd"), 2)
            for t in range(S):
                v = xs0[:, t * D:(t + 1) * D]
                last = nc.scalar.activation(v, v, ACT.Relu, bias=nmr0[:, t:t + 1], scale=rstd0[:, t:t + 1])
            last.then_inc(sem("n_relu"), 1)
            act.wait_ge(sem("n_relu"), 1)
            nc.scalar.activation(h0v[:, :, 0, :], tiles(xs0, D), ACT.Copy).then_inc(sem("n_high"), 1)
            branch(act, act_layers)

        @block.tensor
        def _(pe):
            pe.wait_ge(sem("ones"), 3)
            pe.wait_ge(sem("ident"), 2)
            pe.wait_ge(sem("diag"), 1)
            nc.tensor.matmul(bank(0, ER, P), onesf[0:ER, 0:P], diag, start=True, stop=True).then_inc(sem("firsts"), 1)
            pe.wait_ge(sem("w_in"), 16 * NW)
            blocks = []
            for name in ("l0", "r0", "l1", "r1", "a", "b"):
                at, kt, mt = WN[name]
                for k in range(kt):
                    for m in range(mt):
                        blocks.append(wn[:, at + (m * kt + k) * 128:at + (m * kt + k) * 128 + 128])
            for n, b in enumerate(blocks):
                if n == 16:
                    pe.wait_ge(sem("wt"), 1)
                last = nc.tensor.transpose(bank(4 + (n // 4) % 4)[:, (n % 4) * 128:(n % 4) * 128 + 128], b, identf[:])
                if n % 4 == 3 or n == len(blocks) - 1:
                    last.then_inc(sem("wturned"), 1)
            pe.wait_ge(sem("absw"), 1)
            pe.wait_ge(sem("rowi"), 1)
            for m in range(2):
                for k in range(2):
                    last = nc.tensor.matmul(bank(0)[:, m:m + 1], absw[:, k * 256 + m * 128:k * 256 + m * 128 + 128], ones_c,
                                            start=(k == 0), stop=(k == 1))
            last.then_inc(sem("bound1"), 1)
            pe.wait_ge(sem("bound1s"), 1)
            for m in range(2):
                last = nc.tensor.matmul(bank(0)[:, 2:3], absw[:, 512 + m * 128:640 + m * 128], bnd[:, m:m + 1],
                                        start=(m == 0), stop=(m == 1))
            last.then_inc(sem("boundz"), 1)
            for g in range(QG):
                pe.wait_ge(sem("relative"), g + 1)
                at = 2 * BANK + g * P if g < 4 else 3 * BANK
                last = nc.tensor.transpose(ps[:, at:at + P], gk[:, g * CAP:(g + 1) * CAP], identf[0:P, 0:P])
            last.then_inc(sem("keysT"), 1)
            pe.wait_ge(sem("held"), 1)
            nc.tensor.matmul(bank(1, 1, 1), flag_f, onesf[:, 0:1], start=True, stop=True).then_inc(sem("held_sum"), 1)
            pe.wait_ge(sem("below"), 1)
            pe.wait_ge(sem("wt"), 4)
            for g in range(QG):
                for j in range(WD + 1):
                    last = nc.tensor.matmul(bank(7, QG * (WD + 1), P)[:, g * (WD + 1) + j:g * (WD + 1) + j + 1],
                                            below[j][:, g * P:(g + 1) * P], ones_h, start=True, stop=True)
            last.then_inc(sem("below_sums"), 1)
            branch(pe, pe_layers)


_INS = ["x", "src", "dst", "L0_gnn_W1", "L0_gnn_b1", "L0_gnn_W2", "L0_gnn_b2", "L1_gnn_W_l0", "L1_gnn_b_l0", "L1_gnn_W_r0",
        "L1_gnn_W_l1", "L1_gnn_b_l1", "L1_gnn_W_r1", "L1_gnn_W_lin1", "L1_gnn_b_lin1", "L1_gnn_W_lin2", "L1_gnn_b_lin2"]


def kernel(**inputs):
    import numpy as _np
    import concourse.bacc as _bacc
    from concourse import mybir as _mybir
    from concourse.bass_utils import run_bass_kernel_spmd as _run

    nc = _bacc.Bacc("TRN2", target_bir_lowering=False, num_devices=1)
    arrays, args = {}, []
    for name in _INS:
        a = _np.ascontiguousarray(inputs[name])
        arrays[f"in_{name}_dram"] = a
        args.append(nc.dram_tensor(f"in_{name}_dram", a.shape, _mybir.dt.from_np(a.dtype), kind="ExternalInput").ap())
    out = nc.dram_tensor("out_0_dram", (N, D), _mybir.dt.float32, kind="ExternalOutput").ap()
    sage_program(nc, *args, out)
    r = _run(nc, [arrays], core_ids=[0])
    return r.results[0]["out_0_dram"]
```
